# Optimizing a Trainium2 kernel written in Bass

```python
import numpy as np
import jax
import jax.numpy as jnp

def _softmax(x, axis=-1):
    return jax.nn.softmax(x, axis=axis)

def _gelu(x):
    return jax.nn.gelu(x, approximate=True)

def _silu(x):
    return jax.nn.silu(x)

def _sigmoid(x):
    return jax.nn.sigmoid(x)

def _layernorm(x, axis=-1, eps=1e-05):
    m = jnp.mean(x, axis=axis, keepdims=True)
    v = jnp.var(x, axis=axis, keepdims=True)
    return (x - m) / jnp.sqrt(v + eps)

def _scatter_add(tgt, idx, src, axis=0):
    return tgt.at[idx].add(src)

def _segment_sum(src, seg, n):
    return jax.ops.segment_sum(src, seg, n)
kernel_name = 'mk_xattn_ffn_d1_seqx_r8_d9cb2f'

def setup_inputs(seed: int=0):
    np.random.seed(seed)
    _w = jnp.asarray

    def _rec_inputs():
        import jax
        import jax.numpy as jnp
        _rk = jax.random.key(seed)
        x = -0.000125 + 0.9999 * jax.random.normal(jax.random.fold_in(_rk, 1), (16, 128, 256), jnp.float32)
        _lenS = 128 - jax.random.randint(jax.random.fold_in(_rk, 7), (16,), 0, max(1, 128 // 4) + 1, jnp.int32)
        _lenS2 = 128 - jax.random.randint(jax.random.fold_in(_rk, 8), (16,), 0, max(1, 128 // 4) + 1, jnp.int32)
        _ctx_2048P = jax.random.normal(jax.random.fold_in(_rk, 11), (16, 16, 256), jnp.float32)
        _ctx_2048c = jax.random.dirichlet(jax.random.fold_in(_rk, 511), 0.3 * jnp.ones((16,), jnp.float32), (16, 128))
        _ctx_2048t = jnp.einsum('bsk,bkd->bsd', _ctx_2048c, _ctx_2048P)
        _ctx_2048t = _ctx_2048t * jax.lax.rsqrt(jnp.mean(jnp.square(_ctx_2048t)) + 1e-12) * 0.953939
        ctx_2048 = -1.52775e-05 + 0.999936 * (_ctx_2048t + 0.3 * jax.random.normal(jax.random.fold_in(_rk, 611), (16, 128, 256), jnp.float32))
        _validS = jnp.arange(128)[None, :] < _lenS[:, None]
        _validS2 = jnp.arange(128)[None, :] < _lenS2[:, None]
        _causal = jnp.tril(jnp.ones((128, 128), dtype=bool))
        mask_BxS2_ff1 = jnp.where(jnp.ones((16, 128), dtype=bool), 1.0, 0.0).astype(jnp.float32)
        return (x, ctx_2048, mask_BxS2_ff1)
    x, ctx_2048, mask_BxS2_ff1 = _rec_inputs()

    def _L0_xattn_setup():
        import jax, jax.numpy as jnp
        import numpy as np
        H = 256
        NH = 16
        HD = H // NH
        FD = 64
        key = jax.random.key(seed)
        ks = jax.random.split(key, 12)
        B, S = (4, 512)
        s = 1.0 / np.sqrt(H)
        sf = 1.0 / np.sqrt(HD)
        return {'query': jax.random.normal(ks[0], (B, S, H), jnp.float32), 'key': jax.random.normal(ks[1], (B, S, H), jnp.float32), 'value': jax.random.normal(ks[2], (B, S, H), jnp.float32), 'attention_mask': jnp.ones((B, S), jnp.float32), 'Wq': jax.random.normal(ks[3], (H, H), jnp.float32) * s, 'bq': jnp.zeros((H,), jnp.float32), 'Wk': jax.random.normal(ks[4], (H, H), jnp.float32) * s, 'bk': jnp.zeros((H,), jnp.float32), 'Wv': jax.random.normal(ks[5], (H, H), jnp.float32) * s, 'bv': jnp.zeros((H,), jnp.float32), 'Wqf': jax.random.normal(ks[6], (FD, HD), jnp.float32) * sf, 'Wkf': jax.random.normal(ks[7], (FD, HD), jnp.float32) * sf, 'Wo': jax.random.normal(ks[8], (H, H), jnp.float32) * s, 'bo': jnp.zeros((H,), jnp.float32)}
    _L0_xattn_all = _L0_xattn_setup()
    _L0_xattn_in = {k: v for k, v in _L0_xattn_all.items() if k in ('Wq', 'bq', 'Wk', 'bk', 'Wv', 'bv', 'Wqf', 'Wkf', 'Wo', 'bo')}
    del _L0_xattn_all

    def _L0_ffn_setup():
        import jax, jax.numpy as jnp
        import numpy as np
        E = 8
        TOP_K = 2
        D = 256
        M = 896
        B, S = (2, 256)
        key = jax.random.key(seed)
        kx, kg, k1, k2, k3 = jax.random.split(key, 5)
        x = jax.random.normal(kx, (B, S, D), dtype=jnp.float32)
        gate_w = jax.random.normal(kg, (D, E), dtype=jnp.float32) / np.sqrt(D)
        w1 = jax.random.normal(k1, (E, D, M), dtype=jnp.float32) / np.sqrt(D)
        w2 = jax.random.normal(k2, (E, M, D), dtype=jnp.float32) / np.sqrt(M)
        w3 = jax.random.normal(k3, (E, D, M), dtype=jnp.float32) / np.sqrt(D)
        return {'x': x, 'gate_w': gate_w, 'w1': w1, 'w2': w2, 'w3': w3}
    _L0_ffn_all = _L0_ffn_setup()
    _L0_ffn_in = {k: v for k, v in _L0_ffn_all.items() if k in ('gate_w', 'w1', 'w2', 'w3')}
    del _L0_ffn_all
    return {'x': x, 'ctx_2048': ctx_2048, 'mask_BxS2_ff1': mask_BxS2_ff1, 'L0_xattn_Wq': _L0_xattn_in['Wq'], 'L0_xattn_bq': _L0_xattn_in['bq'], 'L0_xattn_Wk': _L0_xattn_in['Wk'], 'L0_xattn_bk': _L0_xattn_in['bk'], 'L0_xattn_Wv': _L0_xattn_in['Wv'], 'L0_xattn_bv': _L0_xattn_in['bv'], 'L0_xattn_Wqf': _L0_xattn_in['Wqf'], 'L0_xattn_Wkf': _L0_xattn_in['Wkf'], 'L0_xattn_Wo': _L0_xattn_in['Wo'], 'L0_xattn_bo': _L0_xattn_in['bo'], 'L0_ffn_gate_w': _L0_ffn_in['gate_w'], 'L0_ffn_w1': _L0_ffn_in['w1'], 'L0_ffn_w2': _L0_ffn_in['w2'], 'L0_ffn_w3': _L0_ffn_in['w3']}

def reference(x, ctx_2048, mask_BxS2_ff1, L0_xattn_Wq, L0_xattn_bq, L0_xattn_Wk, L0_xattn_bk, L0_xattn_Wv, L0_xattn_bv, L0_xattn_Wqf, L0_xattn_Wkf, L0_xattn_Wo, L0_xattn_bo, L0_ffn_gate_w, L0_ffn_w1, L0_ffn_w2, L0_ffn_w3):
    import jax
    import jax.numpy as jnp

    def _L0_xattn_ref(query, key, value, attention_mask, Wq, bq, Wk, bk, Wv, bv, Wqf, Wkf, Wo, bo):
        import jax, jax.numpy as jnp
        import numpy as np
        H = 256
        NH = 16
        HD = H // NH
        FD = 64
        B, Sq, _ = query.shape
        Sk = key.shape[1]

        def heads(x, W, b, S):
            return (x @ W.T + b).reshape(B, S, NH, HD).transpose(0, 2, 1, 3)
        q = heads(query, Wq, bq, Sq)
        k = heads(key, Wk, bk, Sk)
        v = heads(value, Wv, bv, Sk)
        q_prime = jax.nn.relu(jnp.einsum('bhnd,fd->bhnf', q, Wqf))
        k_prime = jax.nn.relu(jnp.einsum('bhnd,fd->bhnf', k, Wkf))
        k_prime = k_prime * attention_mask[:, None, :, None]
        kv = jnp.einsum('bhnf,bhne->bhfe', k_prime, v)
        qkv = jnp.einsum('bhmf,bhfe->bhme', q_prime, kv)
        k_sum = jnp.sum(k_prime, axis=2)
        qk_sum = jnp.einsum('bhmf,bhf->bhm', q_prime, k_sum)[..., None]
        out = qkv / (qk_sum + 1e-08)
        out = out.transpose(0, 2, 1, 3).reshape(B, Sq, H)
        return out @ Wo.T + bo

    def _L0_ffn_ref(x, gate_w, w1, w2, w3):
        import jax, jax.numpy as jnp
        import numpy as np
        E = 8
        TOP_K = 2
        D = 256
        M = 896
        B, S = (2, 256)
        b, s, d = x.shape
        x_flat = x.reshape(-1, d)
        router_logits = x_flat @ gate_w
        router_probs = jax.nn.softmax(router_logits, axis=-1)
        topk_w, topk_idx = jax.lax.top_k(router_probs, TOP_K)
        topk_w = topk_w / jnp.sum(topk_w, axis=-1, keepdims=True)
        idx_flat = topk_idx.reshape(-1)
        sort_idx = jnp.argsort(idx_flat)
        x_rep_sort = jnp.take(x_flat, sort_idx // TOP_K, axis=0)
        group_sizes = jnp.bincount(idx_flat, length=E).astype(jnp.int32)
        h = jax.lax.ragged_dot(x_rep_sort, w1, group_sizes)
        h = jax.nn.silu(h) * jax.lax.ragged_dot(x_rep_sort, w3, group_sizes)
        out_sort = jax.lax.ragged_dot(h, w2, group_sizes)
        inv_sort_idx = jnp.argsort(sort_idx)
        out_rep = jnp.take(out_sort, inv_sort_idx, axis=0).reshape(-1, TOP_K, d)
        out = jnp.einsum('tkd,tk->td', out_rep, topk_w)
        return out.reshape(b, s, d)
    x = x + _L0_xattn_ref(_layernorm(x, axis=-1), ctx_2048, ctx_2048, mask_BxS2_ff1, L0_xattn_Wq, L0_xattn_bq, L0_xattn_Wk, L0_xattn_bk, L0_xattn_Wv, L0_xattn_bv, L0_xattn_Wqf, L0_xattn_Wkf, L0_xattn_Wo, L0_xattn_bo)
    x = x + _L0_ffn_ref(_layernorm(x, axis=-1), L0_ffn_gate_w, L0_ffn_w1, L0_ffn_w2, L0_ffn_w3)
    return x

_drawn_inputs = setup_inputs


def setup_inputs(seed=0):
    import zlib

    import numpy as np

    out = dict(_drawn_inputs(seed))
    spreads = {'L0_xattn_bq': (0.0, 0.308),
     'L0_xattn_bk': (0.0, 0.4),
     'L0_xattn_bv': (0.0, 0.1),
     'L0_xattn_bo': (0.0, 0.1)}
    factors = {}
    for name, (base, spread) in spreads.items():
        noise = np.random.default_rng([zlib.crc32(name.encode()), seed]).standard_normal(out[name].shape)
        drawn = base * np.exp(spread * noise) if base else spread * noise
        out[name] = jnp.asarray(drawn.astype(out[name].dtype))
    for name, factor in factors.items():
        out[name] = (out[name] * factor).astype(out[name].dtype)
    return out
```

```python
from contextlib import ExitStack

import concourse.bass as bass
from concourse import mybir

P = 128
T, D = 2048, 256
NT = T // P
KD = D // P
NH, HD, FD = 16, 16, 64
HALF = NH * FD // KD
PAIRS = NH // 2
AUG = HD + 1
E, M = 8, 896
MB = M // P
MC = M // 2
ROW = D + 2
CAP = T + P
PAD_AT = E * CAP
TILES = 2 * T // P + E - 1
W13, W2 = KD * M, MB * D
WALL = 2 * W13 + W2
EPS = 1e-5

F32 = mybir.dt.float32
F32R = mybir.dt.float32r
BF16 = mybir.dt.bfloat16
I32 = mybir.dt.int32
U32 = mybir.dt.uint32
ALU = mybir.AluOpType
ACT = mybir.ActivationFunctionType
AX = mybir.AxisListType


def build(nc, x, ctx, maskT, wqT, bq, wkT, bk, wvT, bv, bdq, bdk, woT, bo, gate, w1, w2, w3, out):
    bucket = nc.dram_tensor("bucket", [PAD_AT + P, ROW], F32, kind="Internal").ap()

    with ExitStack() as stack:
        def sb(name, shape, dt=F32):
            return stack.enter_context(nc.sbuf_tensor(name, shape, dt))

        def sem(name):
            return stack.enter_context(nc.semaphore(name))

        bank = [stack.enter_context(nc.psum_tensor(f"bank{i}", [P, 512], F32)) for i in range(8)]

        raw = sb("raw", [P, 2 * WALL])
        w_hi = sb("w_hi", [P, 2 * WALL], F32R)
        w_lo = sb("w_lo", [P, 2 * WALL], F32R)
        ident = sb("ident", [P, P])
        ones = sb("ones", [P, P], BF16)
        before = sb("before", [P, P], BF16)
        expert_no = sb("expert_no", [P, E])
        expert_base = sb("expert_base", [P, E])
        token_id = sb("token_id", [P, NT], U32)
        minus_half = sb("minus_half", [P, NT])
        pad_rows = sb("pad_rows", [P, ROW])
        wq_s, wk_s, wv_s, wo_s = (sb(n, [P, KD, D]) for n in ("wq_s", "wk_s", "wv_s", "wo_s"))
        bdq_s, bdk_s = sb("bdq_s", [P, HALF]), sb("bdk_s", [P, HALF])
        bq_s, bk_s = sb("bq_s", [P, KD]), sb("bk_s", [P, KD])
        bv_s, bo_s = sb("bv_s", [P, D]), sb("bo_s", [P, D])
        gate_s = sb("gate_s", [P, KD, E])
        mask_s = sb("mask_s", [P, NT])
        x_all = sb("x_all", [P, NT * D])
        c_in = sb("c_in", [P, D])
        stats = sb("stats", [P, NT, 6])
        mv = sb("mv", [P, NT, 2])
        rs1 = sb("rs1", [P, 5, NT])
        xn = sb("xn", [P, D])
        xcT = sb("xcT", [P, 2 * KD, P])
        qT, kT = sb("qT", [P, KD, P]), sb("kT", [P, KD, P])
        v_aug = sb("v_aug", [P, NH, AUG])
        qf, kf = sb("qf", [P, NH * FD]), sb("kf", [P, NH * FD])
        kv = sb("kv", [P, PAIRS, 2 * AUG])
        den = sb("den", [P, NH])
        rden = sb("rden", [P, NH])
        att = sb("att", [P, NH, HD])
        attT = sb("attT", [P, KD, P])
        xb = sb("xb", [P, D])
        x2 = sb("x2", [P, D])
        stats2 = sb("stats2", [P, 6])
        mv2 = sb("mv2", [P, 2])
        rs2 = sb("rs2", [P, 5])
        rows = sb("rows", [P, 2, ROW])
        x2T = sb("x2T", [P, KD, P])
        neg_max = sb("neg_max", [P, 1])
        ex = sb("ex", [P, E])
        ex_sum = sb("ex_sum", [P, 1])
        inv_sum = sb("inv_sum", [P, 1])
        prob = sb("prob", [P, E])
        best = sb("best", [P, 8])
        best_i = sb("best_i", [P, 8], U32)
        best_f = sb("best_f", [P, 2])
        top_sum = sb("top_sum", [P, 1])
        inv_top = sb("inv_top", [P, 1])
        pick = sb("pick", [P, 2, E])
        chosen = sb("chosen", [P, E], BF16)
        counted = sb("counted", [P, E], BF16)
        slot_of = sb("slot_of", [P, E])
        picked = sb("picked", [P, 2, E])
        slot_f = sb("slot_f", [P, 2])
        slot = sb("slot", [P, 2], U32)
        steps = sb("steps", [1, E, NT])
        tile_no = sb("tile_no", [1, TILES, E])
        n_row = sb("n_row", [1, E])
        more = sb("more", [1, E, NT])
        n_tiles = sb("n_tiles", [1, E])
        ends = sb("ends", [1, 4, E])
        past = sb("past", [1, TILES, E])
        skip = sb("skip", [1, TILES, E])
        lists = sb("lists", [1, 5, TILES])
        tab_row = sb("tab_row", [1, TILES], I32)
        tab_expert = sb("tab_expert", [1, TILES], I32)
        tab_first = sb("tab_first", [1, TILES], I32)
        tab_count = sb("tab_count", [1, E], I32)
        meta = sb("meta", [P, 4, 2])
        x_hi, x_lo = sb("x_hi", [P, KD, P], F32R), sb("x_lo", [P, KD, P], F32R)
        g_hi, g_lo = sb("g_hi", [P, MB, P], F32R), sb("g_lo", [P, MB, P], F32R)
        y = x_all[:, 0:4 * D].rearrange("p (u d) -> p u d", u=4)
        silu = x_all[:, 4 * D:4 * D + M].rearrange("p (c m) -> p c m", c=2)
        g = x_all[:, 4 * D + M:4 * D + 2 * M]
        x_in = x_all[:, 4 * D + 2 * M:4 * D + 2 * M + 4 * ROW].rearrange("p (u d) -> p u d", u=4)

        x_loaded = [sem(f"x_loaded{i}") for i in range(4)]
        att_w_loaded, out_w_loaded, c_loaded = sem("att_w_loaded"), sem("out_w_loaded"), sem("c_loaded")
        raw_loaded = [sem("raw_loaded0"), sem("raw_loaded1")]
        raw_ready, hi_ready, expert_ready = sem("raw_ready"), sem("hi_ready"), sem("expert_ready")
        consts_ready, zeroed = sem("consts_ready"), sem("zeroed")
        stats_ready, mv_ready, rs1_step, xn_ready = sem("stats_ready"), sem("mv_ready"), sem("rs1_step"), sem("xn_ready")
        tr_done, xcT_ready = sem("tr_done"), sem("xcT_ready")
        k_done, q_done, v_done = sem("k_done"), sem("q_done"), sem("v_done")
        kT_ready, qT_ready, v_ready = sem("kT_ready"), sem("qT_ready"), sem("v_ready")
        kf_done, qf_done, kf_ready, qf_ready = sem("kf_done"), sem("qf_done"), sem("kf_ready"), sem("qf_ready")
        kv_done, kv_ready, qkv_done = sem("kv_done"), sem("kv_ready"), sem("qkv_done")
        den_step, att_ready = sem("den_step"), sem("att_ready")
        attT_done, attT_ready, proj_done = sem("attT_done"), sem("attT_ready"), sem("proj_done")
        xb_ready, x2_ready, x2_stored = sem("xb_ready"), sem("x2_ready"), sem("x2_stored")
        stats2_ready, mv2_ready, rs2_step = sem("stats2_ready"), sem("mv2_ready"), sem("rs2_step")
        rows0_ready, rows1_ready = sem("rows0_ready"), sem("rows1_ready")
        x2T_done, x2T_ready, logits_done = sem("x2T_done"), sem("x2T_ready"), sem("logits_done")
        max_ready, exp_ready, top_step, chosen_ready = sem("max_ready"), sem("exp_ready"), sem("top_step"), sem("chosen_ready")
        rank_done, slot_step, slot_ready, scattered = sem("rank_done"), sem("slot_step"), sem("slot_ready"), sem("scattered")
        counts_done, list_step, list_ready, pads_stored = sem("counts_done"), sem("list_step"), sem("list_ready"), sem("pads_stored")
        gate_pass = sem("gate_pass")
        x_in_loaded = [sem(f"x_in_loaded{i}") for i in range(4)]
        xT_done, x_hi_ready, x_lo_ready = sem("xT_done"), sem("x_hi_ready"), sem("x_lo_ready")
        h_done, silu_ready, g_ready = sem("h_done"), sem("silu_ready"), sem("g_ready")
        gT_done, g_hi_ready, g_lo_ready = sem("gT_done"), sem("g_hi_ready"), sem("g_lo_ready")
        y_done, y_ready, y_added, meta_ready = sem("y_done"), sem("y_ready"), sem("y_added"), sem("meta_ready")

        def settle(eng):
            eng.sem_inc(gate_pass, 1)

        def steps_of_attention(eng, step):
            step(0)
            step(1)
            with eng.Fori(2, NT - 2) as s:
                step(s)
            for s in range(NT - 2, NT + 2):
                step(s)

        def live(s, ahead):
            return not isinstance(s, int) or 0 <= s + ahead < NT

        def tile_live(t, ahead):
            return not isinstance(t, int) or 0 <= t + ahead < TILES

        def weight_rows(e):
            return (
                (0, W13, w1[e].rearrange("(k p) m -> p k m", p=P), M),
                (W13, W13, w3[e].rearrange("(k p) m -> p k m", p=P), M),
                (2 * W13, W2, w2[e].rearrange("(k p) m -> p k m", p=P), D),
            )

        block = stack.enter_context(nc.Block())

        @block.sync
        def _(sp):
            def load_expert(e):
                for at, n, src, width in weight_rows(e):
                    dst = raw[:, (e % 2) * WALL + at:(e % 2) * WALL + at + n]
                    sp.dma_start(dst.rearrange("p (k m) -> p k m", m=width), src).then_inc(raw_loaded[e % 2], 16)

            for i in range(4):
                w = NT // 4 * D
                src = x[i * (T // 4):(i + 1) * (T // 4), :].rearrange("(n p) d -> p n d", p=P)
                sp.dma_start(x_all[:, i * w:(i + 1) * w].rearrange("p (n d) -> p n d", d=D), src).then_inc(x_loaded[i], 16)
                if i == 0:
                    sp.dma_start(c_in[:], ctx[0:P, :]).then_inc(c_loaded, 16)
                    for dst, src in ((wk_s, wkT), (wq_s, wqT), (wv_s, wvT)):
                        sp.dma_start(dst[:], src.rearrange("(k p) n -> p k n", p=P)).then_inc(att_w_loaded, 16)
                    for dst, src in ((bk_s, bk), (bq_s, bq)):
                        sp.dma_start(dst[:], src).then_inc(att_w_loaded, 16)
                    sp.dma_start(bv_s[:], bv.to_broadcast([P, D])).then_inc(att_w_loaded, 16)
                    sp.dma_start(mask_s[:], maskT).then_inc(att_w_loaded, 16)
                    for dst, src in ((bdk_s, bdk), (bdq_s, bdq)):
                        sp.dma_start(dst[:], src).then_inc(att_w_loaded, 16)
            sp.dma_start(wo_s[:], woT.rearrange("(k p) n -> p k n", p=P)).then_inc(out_w_loaded, 16)
            sp.dma_start(gate_s[:], gate.rearrange("(k p) n -> p k n", p=P)).then_inc(out_w_loaded, 16)
            sp.dma_start(bo_s[:], bo.to_broadcast([P, D])).then_inc(out_w_loaded, 16)
            load_expert(0)
            load_expert(1)
            sp.wait_ge(consts_ready, 1)
            sp.dma_start(out[T:T + P, :], pad_rows[:, 0:D]).then_inc(x2_stored, 16)
            sp.dma_start(bucket[PAD_AT:PAD_AT + P, :], pad_rows[:]).then_inc(pads_stored, 16)
            for e in range(2):
                sp.wait_ge(raw_loaded[e], 48)
                sp.sem_inc(raw_ready, 1)

            def step(s):
                if live(s, 1):
                    sp.wait_ge(tr_done, s + 1)
                    sp.dma_start(c_in[:], ctx[bass.ds((s + 1) * P, P), :]).then_inc(c_loaded, 16)
                if live(s, -1):
                    sp.wait_ge(x2_ready, s)
                    sp.dma_start(out[bass.ds((s - 1) * P, P), :], x2[:]).then_inc(x2_stored, 16)

            steps_of_attention(sp, step)
            sp.wait_ge(list_ready, 4)
            for e in range(E):
                n = sp.value_load(tab_count[0:1, e:e + 1], min_val=0, max_val=T)
                sp.dma_start(bucket[bass.ds(n + e * CAP, P), :], pad_rows[:]).then_inc(pads_stored, 16)
            for e in range(2, E):
                sp.wait_ge(expert_ready, e - 1)
                load_expert(e)
                sp.wait_ge(raw_loaded[e % 2], 48 * (e // 2 + 1))
                sp.sem_inc(raw_ready, 1)

        @block.gpsimd
        def _(pool):
            pool.memset(pad_rows[:], 0.0).then_inc(zeroed, 1)
            pool.memset(ident[:], 0.0).then_inc(zeroed, 1)
            pool.memset(before[:], 0.0).then_inc(zeroed, 1)
            pool.memset(ones[:], 1.0)
            pool.memset(kv[:], 0.0)
            pool.memset(counted[:], 0.0)
            pool.memset(minus_half[:], -0.5)
            pool.memset(v_aug[:], 1.0)
            pool.wait_ge(zeroed, 1)
            pool.iota(pad_rows[:, D:D + 1].bitcast(U32), pattern=[[0, 1]], base=T, channel_multiplier=1).then_inc(consts_ready, 1)
            pool.wait_ge(zeroed, 3)
            pool.affine_select(out=ident[:], in_=ident[:], compare_op=ALU.not_equal, fill=1.0, base=0,
                               pattern=[[-1, P]], channel_multiplier=1)
            pool.affine_select(out=before[:], in_=before[:], compare_op=ALU.is_ge, fill=1.0, base=0,
                               pattern=[[-1, P]], channel_multiplier=1)
            pool.iota(token_id[:], pattern=[[P, NT]], base=0, channel_multiplier=1)
            pool.iota(expert_no[:], pattern=[[1, E]], base=0, channel_multiplier=0, allow_small_or_imprecise_dtypes=True)
            pool.iota(expert_base[:], pattern=[[CAP, E]], base=0, channel_multiplier=0, allow_small_or_imprecise_dtypes=True)
            pool.iota(steps[:], pattern=[[0, E], [P, NT]], base=0, channel_multiplier=0, allow_small_or_imprecise_dtypes=True)
            pool.iota(tile_no[:], pattern=[[1, TILES], [0, E]], base=0, channel_multiplier=0,
                      allow_small_or_imprecise_dtypes=True).then_inc(consts_ready, 1)

            def inverse_root(r, var, half, step_sem, done):
                pool.tensor_scalar(r[0], var, EPS, None, ALU.add).then_inc(step_sem, 1)
                pool.wait_ge(step_sem, done + 1)
                pool.tensor_tensor(r[1], r[0], half, ALU.pow).then_inc(step_sem, 1)
                pool.wait_ge(step_sem, done + 2)
                pool.tensor_tensor(r[2], r[1], r[1], ALU.mult).then_inc(step_sem, 1)
                pool.wait_ge(step_sem, done + 3)
                pool.tensor_tensor(r[3], r[2], r[0], ALU.mult).then_inc(step_sem, 1)
                pool.wait_ge(step_sem, done + 4)
                settle(pool)
                pool.tensor_scalar(r[2], r[3], -0.5, 1.5, ALU.mult, ALU.add).then_inc(step_sem, 1)
                pool.wait_ge(step_sem, done + 5)
                pool.tensor_tensor(r[4], r[1], r[2], ALU.mult).then_inc(step_sem, 1)

            pool.wait_ge(consts_ready, 2)
            pool.wait_ge(mv_ready, NT)
            inverse_root([rs1[:, i, :] for i in range(5)], mv[:, :, 1], minus_half[:], rs1_step, 0)
            pool.wait_ge(out_w_loaded, 48)

            def low_halves(e):
                at = (e % 2) * WALL
                for i in range(3):
                    o, n = i * W13, W13
                    pool.wait_ge(hi_ready, 3 * e + (i + 1))
                    last = pool.tensor_tensor(w_lo[:, bass.ds(at + o, n)], raw[:, bass.ds(at + o, n)],
                                              w_hi[:, bass.ds(at + o, n)].bitcast(F32), ALU.subtract)
                last.then_inc(expert_ready, 1)

            def step(s):
                if live(s, -2):
                    pool.wait_ge(rows1_ready, s - 1)
                    pool.wait_ge(slot_ready, s - 1)
                    settle(pool)
                    for k in range(2):
                        pool.indirect_dma_start(out=bucket, out_offset=bass.IndirectOffsetOnAxis(ap=slot[:, k:k + 1], axis=0),
                                                in_=rows[:, k, :], in_offset=None).then_inc(scattered, 16)
                if live(s, -1):
                    pool.wait_ge(mv2_ready, s)
                    settle(pool)
                    inverse_root([rs2[:, i:i + 1] for i in range(5)], mv2[:, 1:2], minus_half[:, 0:1], rs2_step, 6 * (s - 1))
                if live(s, 0):
                    pool.tensor_tensor(xb[:], x_all[:, bass.ds(s * D, D)], bo_s[:], ALU.add).then_inc(xb_ready, 1)
                if isinstance(s, int) and s < 2:
                    low_halves(s)

            steps_of_attention(pool, step)

            pool.wait_ge(x2_stored, 16 * (NT + 1))
            pool.wait_ge(list_ready, 4)
            settle(pool)

            def mix(t, u):
                if tile_live(t, 0) and not (isinstance(t, int) and t == 0):
                    first = pool.value_load(tab_first[0:1, bass.ds(t, 1)], min_val=0, max_val=1)
                    with pool.If(first):
                        e = pool.value_load(tab_expert[0:1, bass.ds(t, 1)], min_val=0, max_val=E - 2)
                        low_halves(e + 1)
                if tile_live(t, -1):
                    pool.wait_ge(y_ready, t)
                    if not (isinstance(t, int) and t == 1):
                        pool.wait_ge(y_added, 16 * (t - 1))
                    settle(pool)
                    v = (u - 1) % 4
                    pool.indirect_dma_start(out=out, out_offset=bass.IndirectOffsetOnAxis(ap=meta[:, v, 0:1].bitcast(U32), axis=0),
                                            in_=y[:, v, :], in_offset=None, compute_op=ALU.add).then_inc(y_added, 16)

            mix(0, 0)
            mix(1, 1)
            rounds = (TILES - 3) // 4
            with pool.Fori(0, rounds) as r:
                for i in range(4):
                    mix(4 * r + (i + 2), (i + 2) % 4)
            for t in range(4 * rounds + 2, TILES + 1):
                mix(t, t % 4)
            pool.wait_ge(y_added, 16 * TILES)

        @block.tensor
        def _(pe):
            def transposes(s):
                pe.wait_ge(xn_ready, s + 1)
                pe.wait_ge(c_loaded, 16 * (s + 1))
                for i, src in enumerate((xn, c_in)):
                    for k in range(KD):
                        last = nc.tensor.transpose(bank[4][:, (KD * i + k) * P:(KD * i + k + 1) * P],
                                                   src[:, k * P:(k + 1) * P], ident[:])
                last.then_inc(tr_done, 1)

            def step(s):
                if live(s, 0):
                    pe.wait_ge(xcT_ready, s + 1)
                    for b, w, at, done in ((1, wk_s, KD, k_done), (0, wq_s, 0, q_done)):
                        for h in range(KD):
                            for k in range(KD):
                                last = nc.tensor.matmul(bank[b][:, h * P:(h + 1) * P], w[:, k, h * P:(h + 1) * P],
                                                        xcT[:, at + k, :], start=(k == 0), stop=(k == KD - 1))
                        last.then_inc(done, 1)
                    for k in range(KD):
                        last = nc.tensor.matmul(bank[2][:, 0:D], xcT[:, KD + k, :], wv_s[:, k, :],
                                                start=(k == 0), stop=(k == KD - 1))
                    last.then_inc(v_done, 1)
                if live(s, -2):
                    pe.wait_ge(chosen_ready, s - 1)
                    nc.tensor.matmul(bank[7][:, 0:E], before[:], chosen[:], start=True, stop=False)
                    nc.tensor.matmul(bank[7][:, 0:E], ones[:], counted[:], start=False, stop=True).then_inc(rank_done, 1)
                if live(s, -1):
                    pe.wait_ge(att_ready, s)
                    for k in range(KD):
                        last = nc.tensor.transpose(bank[3][:, k * P:(k + 1) * P],
                                                   att[:].rearrange("p h d -> p (h d)")[:, k * P:(k + 1) * P], ident[:])
                    last.then_inc(attT_done, 1)
                if live(s, 1):
                    transposes(s + 1)
                if live(s, -1):
                    pe.wait_ge(attT_ready, s)
                    if live(s, -2):
                        pe.wait_ge(exp_ready, s - 1)
                    for k in range(KD):
                        last = nc.tensor.matmul(bank[5][:, 0:D], attT[:, k, :], wo_s[:, k, :],
                                                start=(k == 0), stop=(k == KD - 1))
                    last.then_inc(proj_done, 1)
                if live(s, 0):
                    pe.wait_ge(kT_ready, s + 1)
                    if live(s, -2):
                        pe.wait_ge(slot_ready, s - 1)
                    for h in range(KD):
                        nc.tensor.matmul(bank[6 + h][:], kT[:, h, :], bdk_s[:], start=True, stop=True).then_inc(kf_done, 1)
                    pe.wait_ge(qT_ready, s + 1)
                    for h in range(KD):
                        for j in range(HALF // P):
                            last = nc.tensor.matmul(bank[h][:, j * P:(j + 1) * P], bdq_s[:, j * P:(j + 1) * P],
                                                    qT[:, h, :], start=True, stop=True)
                        last.then_inc(qf_done, 1)
                if live(s, -1):
                    pe.wait_ge(rows0_ready, s)
                    for k in range(KD):
                        last = nc.tensor.transpose(bank[3][:, k * P:(k + 1) * P], rows[:, 0, k * P:(k + 1) * P], ident[:])
                    last.then_inc(x2T_done, 1)
                if live(s, 0):
                    pe.wait_ge(kf_ready, 2 * s + 2)
                    pe.wait_ge(v_ready, s + 1)
                    for j in range(PAIRS):
                        last = nc.tensor.matmul(bank[2][:, j * 2 * AUG:(j + 1) * 2 * AUG], kf[:, j * P:(j + 1) * P],
                                                v_aug[:, 2 * j:2 * j + 2, :], start=True, stop=True)
                    last.then_inc(kv_done, 1)
                if live(s, -1):
                    pe.wait_ge(x2T_ready, s)
                    for k in range(KD):
                        last = nc.tensor.matmul(bank[5][:, 0:E], x2T[:, k, :], gate_s[:, k, :],
                                                start=(k == 0), stop=(k == KD - 1))
                    last.then_inc(logits_done, 1)
                if live(s, 0):
                    pe.wait_ge(qf_ready, 2 * s + 2)
                    pe.wait_ge(kv_ready, 2 * s + 2)
                    for j in range(PAIRS):
                        last = nc.tensor.matmul(bank[6][:, j * 2 * AUG:(j + 1) * 2 * AUG], qf[:, j * P:(j + 1) * P],
                                                kv[:, j, :], start=True, stop=True)
                    last.then_inc(qkv_done, 1)

            pe.wait_ge(consts_ready, 2)
            transposes(0)
            pe.wait_ge(att_w_loaded, 144)
            pe.wait_ge(out_w_loaded, 48)
            steps_of_attention(pe, step)
            pe.wait_ge(slot_ready, NT)
            nc.tensor.matmul(bank[7][:, 0:E], ones[:], counted[:], start=True, stop=True).then_inc(counts_done, 1)
            pe.wait_ge(list_ready, 4)

            def x_transposes(t, u):
                pe.wait_ge(x_in_loaded[u], 16 * (t // 4 + 1))
                for k in range(KD):
                    last = nc.tensor.transpose(bank[7][:, k * P:(k + 1) * P], x_in[:, u, k * P:(k + 1) * P], ident[:])
                last.then_inc(xT_done, 1)

            expert_of = [None]

            def mix(t, u):
                if tile_live(t, 0):
                    before_at = expert_of[0]
                    e = pe.value_load(tab_expert[0:1, bass.ds(t, 1)], min_val=0, max_val=E - 1)
                    now_at = pe.snap((e % 2) * WALL)
                    pe.wait_ge(x_lo_ready, t + 1)
                    pe.wait_ge(expert_ready, e + 1)
                    for c in range(2):
                        for k in range(KD):
                            for part, stationary in enumerate((x_hi, x_lo)):
                                for b, at in ((c, 0), (2 + c, W13)):
                                    for w in ((w_hi, w_lo) if part == 0 else (w_hi,)):
                                        first = k == 0 and part == 0 and w is w_hi
                                        final = k == KD - 1 and part == 1
                                        last = nc.tensor.matmul(bank[b][:, 0:MC], stationary[:, k, :],
                                                                w[:, bass.ds(now_at + (at + k * M + c * MC), MC)],
                                                                start=first, stop=final)
                        last.then_inc(h_done, 1)
                if tile_live(t, -1):
                    if not tile_live(t, 0):
                        e = pe.value_load(tab_expert[0:1, bass.ds(t - 1, 1)], min_val=0, max_val=E - 1)
                        last_at = pe.snap((e % 2) * WALL)
                    else:
                        e = pe.value_load(tab_expert[0:1, bass.ds(t - 1, 1)], min_val=0, max_val=E - 1)
                        last_at = pe.snap((e % 2) * WALL)
                    pe.wait_ge(g_lo_ready, t)
                    if tile_live(t, -2):
                        pe.wait_ge(y_ready, t - 1)
                    for k in range(MB):
                        for part, stationary in enumerate((g_hi, g_lo)):
                            for w in ((w_hi, w_lo) if part == 0 else (w_hi,)):
                                last = nc.tensor.matmul(bank[6][:, 0:D], stationary[:, k, :],
                                                        w[:, bass.ds(last_at + (2 * W13 + k * D), D)],
                                                        start=(k == 0 and part == 0 and w is w_hi),
                                                        stop=(k == MB - 1 and part == 1))
                    last.then_inc(y_done, 1)
                if tile_live(t, 1):
                    x_transposes(t + 1, (u + 1) % 4)
                if tile_live(t, 0):
                    for k in range(MB):
                        if k in (0, MC // P):
                            pe.wait_ge(g_ready, 2 * t + (1 if k == 0 else 2))
                        b, at = (4, k) if k < 4 else (5, k - 4)
                        last = nc.tensor.transpose(bank[b][:, at * P:(at + 1) * P], g[:, k * P:(k + 1) * P], ident[:])
                        if k in (3, MB - 1):
                            last.then_inc(gT_done, 1)

            x_transposes(0, 0)
            mix(0, 0)
            mix(1, 1)
            rounds = (TILES - 3) // 4
            with pe.Fori(0, rounds) as r:
                for i in range(4):
                    mix(4 * r + (i + 2), (i + 2) % 4)
            for t in range(4 * rounds + 2, TILES + 1):
                mix(t, t % 4)

        @block.scalar
        def _(act):
            def evacuate_transposes(s):
                act.wait_ge(tr_done, s + 1)
                nc.scalar.copy(xcT[:].rearrange("p k n -> p (k n)"), bank[4][:]).then_inc(xcT_ready, 1)

            def step(s):
                if live(s, 0):
                    for b, dst, bias, done, ready in ((1, kT, bk_s, k_done, kT_ready), (0, qT, bq_s, q_done, qT_ready)):
                        act.wait_ge(done, s + 1)
                        for h in range(KD):
                            last = nc.scalar.activation(dst[:, h, :], bank[b][:, h * P:(h + 1) * P], ACT.Identity,
                                                        bias=bias[:, h:h + 1])
                        last.then_inc(ready, 1)
                if live(s, -1):
                    act.wait_ge(attT_done, s)
                    nc.scalar.copy(attT[:].rearrange("p k n -> p (k n)"), bank[3][:, 0:D]).then_inc(attT_ready, 1)
                if live(s, 1):
                    evacuate_transposes(s + 1)
                if live(s, 0):
                    for h in range(KD):
                        act.wait_ge(qf_done, 2 * s + (h + 1))
                        nc.scalar.activation(qf[:, h * HALF:(h + 1) * HALF], bank[h][:], ACT.Relu).then_inc(qf_ready, 1)
                if live(s, -1):
                    act.wait_ge(x2T_done, s)
                    nc.scalar.copy(x2T[:].rearrange("p k n -> p (k n)"), bank[3][:, 0:D]).then_inc(x2T_ready, 1)
                    if live(s, -2):
                        act.wait_ge(scattered, 32 * (s - 1))
                    nc.scalar.copy(rows[:, 1, 0:D], rows[:, 0, 0:D]).then_inc(rows1_ready, 1)
                if live(s, 0):
                    act.wait_ge(kv_done, s + 1)
                    for i in range(2):
                        lo = i * FD
                        src = bank[2][lo:lo + FD, 0:PAIRS * 2 * AUG].rearrange("p (j c) -> p j c", c=2 * AUG)
                        nc.scalar.copy(kv[lo:lo + FD, :, i * AUG:(i + 1) * AUG],
                                       src[:, :, i * AUG:(i + 1) * AUG]).then_inc(kv_ready, 1)
                if live(s, -1):
                    act.wait_ge(max_ready, s)
                    nc.scalar.activation(ex[:], bank[5][:, 0:E], ACT.Exp, bias=neg_max[:],
                                         accum_out=ex_sum[:]).then_inc(exp_ready, 1)

            evacuate_transposes(0)
            act.wait_ge(att_w_loaded, 144)
            act.wait_ge(consts_ready, 2)
            steps_of_attention(act, step)

            def load(t, u):
                at = act.value_load(tab_row[0:1, bass.ds(t, 1)], min_val=0, max_val=PAD_AT)
                if tile_live(t, -4):
                    act.wait_ge(meta_ready, t - 3)
                act.dma_start(x_in[:, u, :], bucket[bass.ds(at, P), :]).then_inc(x_in_loaded[u], 16)

            def evacuate_x(t):
                act.wait_ge(xT_done, t + 1)
                nc.scalar.copy(x_hi[:].rearrange("p k n -> p (k n)"), bank[7][:, 0:D]).then_inc(x_hi_ready, 1)

            def mix(t, u):
                if tile_live(t, 2) and not (isinstance(t, int) and t < 2):
                    load(t + 2, (u + 2) % 4)
                if tile_live(t, 0):
                    for c in range(2):
                        act.wait_ge(h_done, 2 * t + (c + 1))
                        nc.scalar.activation(silu[:, c, :], bank[c][:, 0:MC], ACT.Silu).then_inc(silu_ready, 1)
                if tile_live(t, -1):
                    v = (u - 1) % 4
                    act.wait_ge(y_done, t)
                    if tile_live(t, -5):
                        act.wait_ge(y_added, 16 * (t - 4))
                    nc.scalar.activation(y[:, v, :], bank[6][:, 0:D], ACT.Copy, scale=meta[:, v, 1:2]).then_inc(y_ready, 1)
                if tile_live(t, 1):
                    evacuate_x(t + 1)
                if tile_live(t, 0):
                    for i, (b, n) in enumerate(((4, 4), (5, MB - 4))):
                        act.wait_ge(gT_done, 2 * t + (i + 1))
                        nc.scalar.copy(g_hi[:, 4 * i:4 * i + n, :].rearrange("p k n -> p (k n)"),
                                       bank[b][:, 0:n * P]).then_inc(g_hi_ready, 1)

            act.wait_ge(scattered, 32 * NT)
            act.wait_ge(pads_stored, 16 * (E + 1))
            act.wait_ge(list_ready, 4)
            for t in range(4):
                load(t, t)
            evacuate_x(0)
            for t in range(5):
                mix(t, t % 4)
            rounds = (TILES - 7) // 4
            with act.Fori(0, rounds) as r:
                for i in range(4):
                    mix(4 * r + (i + 5), (i + 5) % 4)
            for t in range(4 * rounds + 5, TILES + 1):
                mix(t, t % 4)

        @block.vector
        def _(dve):
            for n in range(NT):
                if n % 4 == 0:
                    dve.wait_ge(x_loaded[n // 4], 16)
                nc.vector.bn_stats(stats[:, n, :], x_all[:, n * D:(n + 1) * D]).then_inc(stats_ready, 1)
            for n in range(NT):
                dve.wait_ge(stats_ready, n + 1)
                nc.vector.bn_aggr(mv[:, n, :], stats[:, n, :]).then_inc(mv_ready, 1)

            def normalise(s):
                nc.vector.tensor_scalar(xn[:], x_all[:, bass.ds(s * D, D)], mv[:, bass.ds(s, 1), 0:1].rearrange("p a b -> p (a b)"),
                                        rs1[:, 4, bass.ds(s, 1)], ALU.subtract, ALU.mult).then_inc(xn_ready, 1)

            def high_halves(e):
                at = (e % 2) * WALL
                for i in range(3):
                    o, n = i * W13, W13
                    nc.vector.tensor_copy(w_hi[:, bass.ds(at + o, n)], raw[:, bass.ds(at + o, n)]).then_inc(hi_ready, 1)

            dve.wait_ge(rs1_step, 6)
            normalise(0)
            dve.wait_ge(tr_done, 1)
            normalise(1)
            dve.wait_ge(att_w_loaded, 144)
            dve.wait_ge(consts_ready, 2)

            def step(s):
                if live(s, 0):
                    dve.wait_ge(v_done, s + 1)
                    nc.vector.tensor_tensor(v_aug[:, :, 0:HD], bank[2][:, 0:D].rearrange("p (h d) -> p h d", d=HD),
                                            bv_s[:].rearrange("p (h d) -> p h d", d=HD), ALU.add).then_inc(v_ready, 1)
                if live(s, -2):
                    dve.wait_ge(rank_done, s - 1)
                    nc.vector.tensor_tensor(slot_of[:], bank[7][:, 0:E], expert_base[:], ALU.add).then_inc(slot_step, 1)
                    nc.vector.tensor_tensor(counted[:], counted[:], chosen[:], ALU.add)
                    dve.wait_ge(slot_step, 3 * (s - 2) + 1)
                    nc.vector.tensor_tensor(picked[:], slot_of[:].rearrange("p (o e) -> p o e", o=1).to_broadcast([P, 2, E]),
                                            pick[:], ALU.mult).then_inc(slot_step, 1)
                    dve.wait_ge(slot_step, 3 * (s - 2) + 2)
                    nc.vector.tensor_reduce(slot_f[:], picked[:], AX.X, ALU.add).then_inc(slot_step, 1)
                    dve.wait_ge(slot_step, 3 * (s - 2) + 3)
                    nc.vector.tensor_copy(slot[:], slot_f[:]).then_inc(slot_ready, 1)
                if live(s, -1):
                    dve.wait_ge(proj_done, s)
                    dve.wait_ge(xb_ready, s)
                    if live(s, -2):
                        dve.wait_ge(x2_stored, 16 * s)
                    nc.vector.tensor_tensor(x2[:], bank[5][:, 0:D], xb[:], ALU.add).then_inc(x2_ready, 1)
                    dve.wait_ge(x2_ready, s)
                    nc.vector.bn_stats(stats2[:], x2[:]).then_inc(stats2_ready, 1)
                    dve.wait_ge(stats2_ready, s)
                    settle(dve)
                    nc.vector.bn_aggr(mv2[:], stats2[:]).then_inc(mv2_ready, 1)
                if live(s, 2):
                    dve.wait_ge(tr_done, s + 2)
                    normalise(s + 2)
                if live(s, 0):
                    for h in range(KD):
                        dve.wait_ge(kf_done, 2 * s + (h + 1))
                        nc.vector.tensor_scalar(kf[:, h * HALF:(h + 1) * HALF], bank[6 + h][:], 0.0,
                                                mask_s[:, bass.ds(s, 1)], ALU.max, ALU.mult).then_inc(kf_ready, 1)
                if live(s, -1):
                    dve.wait_ge(rs2_step, 6 * s)
                    if live(s, -2):
                        dve.wait_ge(scattered, 32 * (s - 1))
                    nc.vector.tensor_scalar(rows[:, 0, 0:D], x2[:], mv2[:, 0:1], rs2[:, 4:5],
                                            ALU.subtract, ALU.mult).then_inc(rows0_ready, 1)
                    dve.wait_ge(logits_done, s)
                    nc.vector.tensor_reduce(neg_max[:], bank[5][:, 0:E], AX.X, ALU.max, negate=True).then_inc(max_ready, 1)
                if live(s, 0):
                    dve.wait_ge(qkv_done, s + 1)
                    o = bank[6][:, 0:NH * AUG].rearrange("p (h c) -> p h c", c=AUG)
                    nc.vector.tensor_scalar(den[:].rearrange("p (h o) -> p h o", o=1), o[:, :, HD:AUG], 1e-8, None,
                                            ALU.add).then_inc(den_step, 1)
                    dve.wait_ge(den_step, 2 * s + 1)
                    nc.vector.reciprocal(rden[:], den[:]).then_inc(den_step, 1)
                    dve.wait_ge(den_step, 2 * s + 2)
                    nc.vector.tensor_tensor(att[:], o[:, :, 0:HD], rden[:].rearrange("p (h o) -> p h o", o=1).to_broadcast([P, NH, HD]),
                                            ALU.mult).then_inc(att_ready, 1)
                if live(s, -1):
                    n = 8 * (s - 1)
                    dve.wait_ge(exp_ready, s)
                    nc.vector.reciprocal(inv_sum[:], ex_sum[:]).then_inc(top_step, 1)
                    dve.wait_ge(top_step, n + 1)
                    nc.vector.tensor_scalar(prob[:], ex[:], inv_sum[:], None, ALU.mult).then_inc(top_step, 1)
                    dve.wait_ge(top_step, n + 2)
                    settle(dve)
                    nc.vector.max(best[:], prob[:]).then_inc(top_step, 1)
                    dve.wait_ge(top_step, n + 3)
                    settle(dve)
                    nc.vector.max_index(best_i[:], best[:], prob[:]).then_inc(top_step, 1)
                    nc.vector.tensor_tensor(top_sum[:], best[:, 0:1], best[:, 1:2], ALU.add).then_inc(top_step, 1)
                    dve.wait_ge(top_step, n + 4)
                    nc.vector.tensor_copy(best_f[:], best_i[:, 0:2]).then_inc(top_step, 1)
                    dve.wait_ge(top_step, n + 5)
                    nc.vector.reciprocal(inv_top[:], top_sum[:]).then_inc(top_step, 1)
                    dve.wait_ge(top_step, n + 6)
                    if live(s, -2):
                        dve.wait_ge(slot_ready, s - 1)
                    for k in range(2):
                        last = nc.vector.tensor_scalar(pick[:, k, :], expert_no[:], best_f[:, k:k + 1], None, ALU.is_equal)
                    last.then_inc(top_step, 1)
                    dve.wait_ge(top_step, n + 7)
                    nc.vector.tensor_scalar(rows[:, :, D + 1:D + 2].rearrange("p k o -> p (k o)"), best[:, 0:2], inv_top[:], None, ALU.mult)
                    nc.vector.tensor_copy(rows[:, :, D:D + 1].rearrange("p k o -> p (k o)").bitcast(U32),
                                          token_id[:, bass.ds(s - 1, 1)].to_broadcast([P, 2]))
                    dve.wait_ge(top_step, n + 8)
                    nc.vector.tensor_tensor(chosen[:], pick[:, 0, :], pick[:, 1, :], ALU.add).then_inc(chosen_ready, 1)
                if isinstance(s, int) and s < 2:
                    dve.wait_ge(raw_ready, s + 1)
                    high_halves(s)

            steps_of_attention(dve, step)

            done = [0]

            def link(ins):
                done[0] += 1
                ins.then_inc(list_step, 1)
                dve.wait_ge(list_step, done[0])

            def wide(a):
                return a.rearrange("a (o e) -> a o e", o=1).to_broadcast([1, TILES, E])

            dve.wait_ge(counts_done, 1)
            link(nc.vector.tensor_copy(n_row[:], bank[7][0:1, 0:E]))
            nc.vector.tensor_copy(tab_count[:], n_row[:]).then_inc(list_ready, 1)
            link(nc.vector.tensor_tensor(more[:], n_row[:].rearrange("a (e o) -> a e o", o=1).to_broadcast([1, E, NT]),
                                         steps[:], ALU.is_gt))
            link(nc.vector.tensor_reduce(n_tiles[:], more[:], AX.X, ALU.add))
            link(nc.vector.tensor_scalar(ends[:, 0, :], n_tiles[:], 1.0, None, ALU.max))
            for i, by in enumerate((1, 2, 4)):
                link(nc.vector.tensor_copy(ends[:, i + 1, 0:by], ends[:, i, 0:by]))
                link(nc.vector.tensor_tensor(ends[:, i + 1, by:E], ends[:, i, by:E], ends[:, i, 0:E - by], ALU.add))
            link(nc.vector.tensor_tensor(past[:], tile_no[:], wide(ends[:, 3, :]), ALU.is_ge))
            link(nc.vector.tensor_reduce(lists[:, 0, :], past[:], AX.X, ALU.add))
            link(nc.vector.tensor_scalar(lists[:, 1, :], lists[:, 0, :], float(E - 1), None, ALU.min))
            nc.vector.tensor_copy(tab_expert[:], lists[:, 1, :]).then_inc(list_ready, 1)
            link(nc.vector.tensor_scalar(n_tiles[:], ends[:, 0, :], -float(P), float(CAP), ALU.mult, ALU.add))
            link(nc.vector.tensor_tensor(skip[:], past[:], wide(n_tiles[:]), ALU.mult))
            link(nc.vector.tensor_reduce(lists[:, 2, :], skip[:], AX.X, ALU.add))
            link(nc.vector.scalar_tensor_tensor(out=lists[:, 3, :], in0=tile_no[:, :, 0], scalar=float(P),
                                                in1=lists[:, 2, :], op0=ALU.mult, op1=ALU.add))
            link(nc.vector.tensor_scalar(lists[:, 3, :], lists[:, 3, :], float(PAD_AT), None, ALU.min))
            nc.vector.tensor_copy(tab_row[:], lists[:, 3, :]).then_inc(list_ready, 1)
            link(nc.vector.memset(lists[:, 4, 0:1], 0.0))
            link(nc.vector.tensor_tensor(lists[:, 4, 1:TILES], lists[:, 1, 1:TILES], lists[:, 1, 0:TILES - 1], ALU.subtract))
            link(nc.vector.tensor_scalar(lists[:, 2, :], lists[:, 1, :], float(E - 1), None, ALU.is_lt))
            link(nc.vector.tensor_tensor(lists[:, 4, :], lists[:, 4, :], lists[:, 2, :], ALU.mult))
            nc.vector.tensor_copy(tab_first[:], lists[:, 4, :]).then_inc(list_ready, 1)
            dve.wait_ge(list_ready, 4)

            def split_x(t, u):
                dve.wait_ge(x_hi_ready, t + 1)
                nc.vector.tensor_tensor(x_lo[:].rearrange("p k n -> p (k n)"), bank[7][:, 0:D],
                                        x_hi[:].rearrange("p k n -> p (k n)").bitcast(F32), ALU.subtract).then_inc(x_lo_ready, 1)
                if tile_live(t, -4):
                    dve.wait_ge(y_added, 16 * (t - 3))
                nc.vector.tensor_copy(meta[:, u, :].bitcast(U32), x_in[:, u, D:ROW].bitcast(U32)).then_inc(meta_ready, 1)

            def mix(t, u):
                if tile_live(t, 0):
                    for c in range(2):
                        dve.wait_ge(silu_ready, 2 * t + (c + 1))
                        nc.vector.tensor_tensor(g[:, c * MC:(c + 1) * MC], bank[2 + c][:, 0:MC], silu[:, c, :],
                                                ALU.mult).then_inc(g_ready, 1)
                if tile_live(t, 1):
                    split_x(t + 1, (u + 1) % 4)
                if tile_live(t, 0):
                    for i, (b, n) in enumerate(((4, 4), (5, MB - 4))):
                        dve.wait_ge(g_hi_ready, 2 * t + (i + 1))
                        last = nc.vector.tensor_tensor(g_lo[:, 4 * i:4 * i + n, :].rearrange("p k n -> p (k n)"),
                                                       bank[b][:, 0:n * P],
                                                       g_hi[:, 4 * i:4 * i + n, :].rearrange("p k n -> p (k n)").bitcast(F32),
                                                       ALU.subtract)
                    last.then_inc(g_lo_ready, 1)
                    if not (isinstance(t, int) and t == 0):
                        first = dve.value_load(tab_first[0:1, bass.ds(t, 1)], min_val=0, max_val=1)
                        with dve.If(first):
                            e = dve.value_load(tab_expert[0:1, bass.ds(t, 1)], min_val=0, max_val=E - 2)
                            dve.wait_ge(y_done, t)
                            dve.wait_ge(raw_ready, e + 2)
                            settle(dve)
                            high_halves(e + 1)

            split_x(0, 0)
            for t in range(4):
                mix(t, t % 4)
            rounds = (TILES - 5) // 4
            with dve.Fori(0, rounds) as r:
                for i in range(4):
                    mix(4 * r + (i + 4), (i + 4) % 4)
            for t in range(4 * rounds + 4, TILES + 1):
                mix(t, t % 4)


def kernel(**inputs):
    import numpy as np
    import concourse.bacc as bacc
    from concourse.bass_utils import run_bass_kernel_spmd as run

    def block_diagonal(w):
        wide = np.zeros((P, HALF), w.dtype)
        for h in range(P // HD):
            wide[h * HD:(h + 1) * HD, h * FD:(h + 1) * FD] = w.T
        return wide

    i = {k: np.asarray(v) for k, v in inputs.items()}
    a = {
        "x": i["x"].reshape(T, D), "ctx": i["ctx_2048"].reshape(T, D), "maskT": i["mask_BxS2_ff1"].T,
        "wqT": i["L0_xattn_Wq"].T, "bq": i["L0_xattn_bq"].reshape(KD, P).T,
        "wkT": i["L0_xattn_Wk"].T, "bk": i["L0_xattn_bk"].reshape(KD, P).T,
        "wvT": i["L0_xattn_Wv"].T, "bv": i["L0_xattn_bv"].reshape(1, D),
        "bdq": block_diagonal(i["L0_xattn_Wqf"]), "bdk": block_diagonal(i["L0_xattn_Wkf"]),
        "woT": i["L0_xattn_Wo"].T, "bo": i["L0_xattn_bo"].reshape(1, D),
        "gate": i["L0_ffn_gate_w"], "w1": i["L0_ffn_w1"], "w2": i["L0_ffn_w2"], "w3": i["L0_ffn_w3"],
    }
    a = {f"in_{k}": np.ascontiguousarray(v) for k, v in a.items()}
    nc = bacc.Bacc("TRN2", target_bir_lowering=False, num_devices=1)
    args = [nc.dram_tensor(k, v.shape, mybir.dt.from_np(v.dtype), kind="ExternalInput").ap() for k, v in a.items()]
    args.append(nc.dram_tensor("out_rows", (T + P, D), F32, kind="ExternalOutput").ap())
    build(nc, *args)
    r = run(nc, [a], core_ids=[0])
    return r.results[0]["out_rows"][0:T].reshape(NT, P, D)
```

```python
from contextlib import ExitStack

import concourse.bass as bass
from concourse import mybir

P = 128
T, D = 2048, 256
NT = T // P
KD = D // P
NH, HD, FD = 16, 16, 64
HALF = NH * FD // KD
PAIRS = NH // 2
AUG = HD + 1
E, M = 8, 896
MB = M // P
MC = M // 2
ROW = D + 2
CAP = T + P
PAD_AT = E * CAP
SURE = 2 * T // P
ROUNDS = SURE // 4 + E // 4
TILES = 4 * ROUNDS + 2
W13, W2 = KD * M, MB * D
WALL = 2 * W13 + W2
PIECE = 2 * WALL // (NT - 4)
EPS = 1e-5

F32 = mybir.dt.float32
F32R = mybir.dt.float32r
BF16 = mybir.dt.bfloat16
I32 = mybir.dt.int32
U32 = mybir.dt.uint32
ALU = mybir.AluOpType
ACT = mybir.ActivationFunctionType
AX = mybir.AxisListType


def build(nc, x, ctx, maskT, wqT, bq, wkT, bk, wvT, bv, bdq, bdk, woT, bo, gate, w1, w2, w3, out):
    bucket = nc.dram_tensor("bucket", [PAD_AT + P, ROW], F32, kind="Internal").ap()

    with ExitStack() as stack:
        def sb(name, shape, dt=F32):
            return stack.enter_context(nc.sbuf_tensor(name, shape, dt))

        def sem(name):
            return stack.enter_context(nc.semaphore(name))

        bank = [stack.enter_context(nc.psum_tensor(f"bank{i}", [P, 512], F32)) for i in range(8)]

        raw = sb("raw", [P, 2 * WALL])
        w_hi = sb("w_hi", [P, 2 * WALL], F32R)
        w_lo = sb("w_lo", [P, 2 * WALL], F32R)
        ident = sb("ident", [P, P])
        ones = sb("ones", [P, P], BF16)
        before = sb("before", [P, P], BF16)
        expert_no = sb("expert_no", [P, E])
        expert_base = sb("expert_base", [P, E])
        token_id = sb("token_id", [P, NT], U32)
        minus_half = sb("minus_half", [P, NT])
        pad_rows = sb("pad_rows", [P, ROW])
        wq_s, wk_s, wv_s, wo_s = (sb(n, [P, KD, D]) for n in ("wq_s", "wk_s", "wv_s", "wo_s"))
        bdq_s, bdk_s = sb("bdq_s", [P, HALF]), sb("bdk_s", [P, HALF])
        bq_s, bk_s = sb("bq_s", [P, KD]), sb("bk_s", [P, KD])
        bv_s, bo_s = sb("bv_s", [P, D]), sb("bo_s", [P, D])
        gate_s = sb("gate_s", [P, KD, E])
        mask_s = sb("mask_s", [P, NT])
        x_all = sb("x_all", [P, NT * D])
        c_in = sb("c_in", [P, D])
        stats = sb("stats", [P, NT, 6])
        mv = sb("mv", [P, NT, 2])
        rs1 = sb("rs1", [P, 5, NT])
        xn = sb("xn", [P, D])
        xcT = sb("xcT", [P, 2 * KD, P])
        qT, kT = sb("qT", [P, KD, P]), sb("kT", [P, KD, P])
        v_aug = sb("v_aug", [P, NH, AUG])
        qf, kf = sb("qf", [P, NH * FD]), sb("kf", [P, NH * FD])
        kv = sb("kv", [P, PAIRS, 2 * AUG])
        den = sb("den", [P, NH])
        rden = sb("rden", [P, NH])
        att = sb("att", [P, NH, HD])
        attT = sb("attT", [P, KD, P])
        xb = sb("xb", [P, D])
        x2 = sb("x2", [P, D])
        stats2 = sb("stats2", [P, 6])
        mv2 = sb("mv2", [P, 2])
        rs2 = sb("rs2", [P, 5])
        xn2 = sb("xn2", [P, D])
        rows = sb("rows", [P, 2, ROW])
        x2T = sb("x2T", [P, KD, P])
        neg_max = sb("neg_max", [P, 1])
        ex = sb("ex", [P, E])
        ex_sum = sb("ex_sum", [P, 1])
        inv_sum = sb("inv_sum", [P, 1])
        prob = sb("prob", [P, E])
        best = sb("best", [P, 8])
        best_i = sb("best_i", [P, 8], U32)
        best_f = sb("best_f", [P, 2])
        top_sum = sb("top_sum", [P, 1])
        inv_top = sb("inv_top", [P, 1])
        pick = sb("pick", [P, 2, E])
        chosen = sb("chosen", [P, E], BF16)
        counted = sb("counted", [P, E], BF16)
        slot_of = sb("slot_of", [P, E])
        picked = sb("picked", [P, 2, E])
        slot_f = sb("slot_f", [P, 2])
        slot = sb("slot", [P, 2], U32)
        steps = sb("steps", [1, E, NT])
        tile_no = sb("tile_no", [1, TILES, E])
        n_row = sb("n_row", [1, E])
        more = sb("more", [1, E, NT])
        n_tiles = sb("n_tiles", [1, E])
        ends = sb("ends", [1, 4, E])
        past = sb("past", [1, TILES, E])
        skip = sb("skip", [1, TILES, E])
        lists = sb("lists", [1, 5, TILES])
        tab_row = sb("tab_row", [1, TILES], I32)
        tab_expert = sb("tab_expert", [1, TILES], I32)
        tab_first = sb("tab_first", [1, TILES], I32)
        tab_count = sb("tab_count", [1, E], I32)
        active = sb("active", [1, ROUNDS])
        used = sb("used", [1, 2])
        tab_active = sb("tab_active", [1, ROUNDS], I32)
        tab_used = sb("tab_used", [1, 1], I32)
        meta = sb("meta", [P, 4, 2])
        x_hi, x_lo = sb("x_hi", [P, KD, P], F32R), sb("x_lo", [P, KD, P], F32R)
        g_hi, g_lo = sb("g_hi", [P, MB, P], F32R), sb("g_lo", [P, MB, P], F32R)
        y = x_all[:, 0:4 * D].rearrange("p (u d) -> p u d", u=4)
        silu = x_all[:, 4 * D:4 * D + M].rearrange("p (c m) -> p c m", c=2)
        g = x_all[:, 4 * D + M:4 * D + 2 * M]
        x_in = x_all[:, 4 * D + 2 * M:4 * D + 2 * M + 4 * ROW].rearrange("p (u d) -> p u d", u=4)

        x_loaded = [sem(f"x_loaded{i}") for i in range(4)]
        att_w_loaded, out_w_loaded, c_loaded = sem("att_w_loaded"), sem("out_w_loaded"), sem("c_loaded")
        raw_loaded = [sem("raw_loaded0"), sem("raw_loaded1")]
        raw_ready, hi_ready, expert_ready = sem("raw_ready"), sem("hi_ready"), sem("expert_ready")
        consts_ready, zeroed = sem("consts_ready"), sem("zeroed")
        stats_ready, mv_ready, rs1_step, xn_ready = sem("stats_ready"), sem("mv_ready"), sem("rs1_step"), sem("xn_ready")
        tr_done, xcT_ready = sem("tr_done"), sem("xcT_ready")
        k_done, q_done, v_done = sem("k_done"), sem("q_done"), sem("v_done")
        kT_ready, qT_ready, v_ready = sem("kT_ready"), sem("qT_ready"), sem("v_ready")
        kf_done, qf_done, kf_ready, qf_ready = sem("kf_done"), sem("qf_done"), sem("kf_ready"), sem("qf_ready")
        kv_done, kv_ready, qkv_done = sem("kv_done"), sem("kv_ready"), sem("qkv_done")
        den_step, att_ready = sem("den_step"), sem("att_ready")
        attT_done, attT_ready, proj_done = sem("attT_done"), sem("attT_ready"), sem("proj_done")
        xb_ready, x2_ready, x2_stored = sem("xb_ready"), sem("x2_ready"), sem("x2_stored")
        stats2_ready, mv2_ready, rs2_step = sem("stats2_ready"), sem("mv2_ready"), sem("rs2_step")
        xn2_ready, rows_ready = sem("xn2_ready"), sem("rows_ready")
        x2T_done, x2T_ready, logits_done = sem("x2T_done"), sem("x2T_ready"), sem("logits_done")
        max_ready, exp_ready, top_step, chosen_ready = sem("max_ready"), sem("exp_ready"), sem("top_step"), sem("chosen_ready")
        rank_done, slot_step, slot_ready, scattered = sem("rank_done"), sem("slot_step"), sem("slot_ready"), sem("scattered")
        counts_done, list_step, list_ready, pads_stored = sem("counts_done"), sem("list_step"), sem("list_ready"), sem("pads_stored")
        pad0_stored = sem("pad0_stored")
        gate_pass = sem("gate_pass")
        x_in_loaded = [sem(f"x_in_loaded{i}") for i in range(4)]
        xT_done, x_hi_ready, x_lo_ready = sem("xT_done"), sem("x_hi_ready"), sem("x_lo_ready")
        h_done, silu_ready, g_ready = sem("h_done"), sem("silu_ready"), sem("g_ready")
        gT_done, g_hi_ready, g_lo_ready = sem("gT_done"), sem("g_hi_ready"), sem("g_lo_ready")
        y_done, y_ready, y_added, meta_ready = sem("y_done"), sem("y_ready"), sem("y_added"), sem("meta_ready")

        def settle(eng):
            eng.sem_inc(gate_pass, 1)

        def steps_of_attention(eng, step, between=None):
            step(0)
            if between:
                between()
            step(1)
            step(2)
            with eng.Fori(3, NT - 3) as s:
                step(s)
            for s in range(NT - 3, NT + 3):
                step(s)

        def live(s, ahead):
            return not isinstance(s, int) or 0 <= s + ahead < NT

        def piece_of(s):
            return s - 2 if not isinstance(s, int) or 2 <= s < NT - 2 else None

        def rounds_of_mixture(eng, step):
            for t in range(8):
                step(t, t % 4)
            with eng.Fori(2, ROUNDS) as r:
                go = eng.value_load(tab_active[0:1, bass.ds(r, 1)], min_val=0, max_val=1)
                with eng.If(go):
                    for i in range(4):
                        step(4 * r + i, i)

        def tile_live(t, ahead):
            return not isinstance(t, int) or t + ahead >= 0

        def tiles_used(eng):
            return eng.value_load(tab_used[0:1, 0:1], min_val=0, max_val=4 * ROUNDS - SURE) + SURE

        def weight_rows(e):
            return (
                (0, W13, w1[e].rearrange("(k p) m -> p k m", p=P), M),
                (W13, W13, w3[e].rearrange("(k p) m -> p k m", p=P), M),
                (2 * W13, W2, w2[e].rearrange("(k p) m -> p k m", p=P), D),
            )

        block = stack.enter_context(nc.Block())

        @block.sync
        def _(sp):
            def load_expert(e):
                for at, n, src, width in weight_rows(e):
                    dst = raw[:, (e % 2) * WALL + at:(e % 2) * WALL + at + n]
                    sp.dma_start(dst.rearrange("p (k m) -> p k m", m=width), src).then_inc(raw_loaded[e % 2], 16)

            for i in range(4):
                w = NT // 4 * D
                src = x[i * (T // 4):(i + 1) * (T // 4), :].rearrange("(n p) d -> p n d", p=P)
                sp.dma_start(x_all[:, i * w:(i + 1) * w].rearrange("p (n d) -> p n d", d=D), src).then_inc(x_loaded[i], 16)
                if i == 0:
                    sp.dma_start(c_in[:], ctx[0:P, :]).then_inc(c_loaded, 16)
                    for dst, src in ((wk_s, wkT), (wq_s, wqT), (wv_s, wvT)):
                        sp.dma_start(dst[:], src.rearrange("(k p) n -> p k n", p=P)).then_inc(att_w_loaded, 16)
                    for dst, src in ((bk_s, bk), (bq_s, bq)):
                        sp.dma_start(dst[:], src).then_inc(att_w_loaded, 16)
                    sp.dma_start(bv_s[:], bv.to_broadcast([P, D])).then_inc(att_w_loaded, 16)
                    sp.dma_start(mask_s[:], maskT).then_inc(att_w_loaded, 16)
                    for dst, src in ((bdk_s, bdk), (bdq_s, bdq)):
                        sp.dma_start(dst[:], src).then_inc(att_w_loaded, 16)
            sp.dma_start(wo_s[:], woT.rearrange("(k p) n -> p k n", p=P)).then_inc(out_w_loaded, 16)
            sp.dma_start(gate_s[:], gate.rearrange("(k p) n -> p k n", p=P)).then_inc(out_w_loaded, 16)
            sp.dma_start(bo_s[:], bo.to_broadcast([P, D])).then_inc(out_w_loaded, 16)
            load_expert(0)
            load_expert(1)
            sp.wait_ge(consts_ready, 1)
            sp.dma_start(out[T:T + P, :], pad_rows[:, 0:D]).then_inc(x2_stored, 16)
            sp.dma_start(bucket[PAD_AT:PAD_AT + P, :], pad_rows[:]).then_inc(pads_stored, 16)
            for e in range(2):
                sp.wait_ge(raw_loaded[e], 48)
                sp.sem_inc(raw_ready, 1)

            def step(s):
                if live(s, 1):
                    sp.wait_ge(tr_done, s + 1)
                    sp.dma_start(c_in[:], ctx[bass.ds((s + 1) * P, P), :]).then_inc(c_loaded, 16)
                if live(s, -1):
                    sp.wait_ge(x2_ready, s)
                    sp.dma_start(out[bass.ds((s - 1) * P, P), :], x2[:]).then_inc(x2_stored, 16)

            steps_of_attention(sp, step)
            sp.wait_ge(list_ready, 1)
            for e in range(E):
                n = sp.value_load(tab_count[0:1, e:e + 1], min_val=0, max_val=T)
                done = pad0_stored if e == 0 else pads_stored
                sp.dma_start(bucket[bass.ds(n + e * CAP, P), :], pad_rows[:]).then_inc(done, 16)
            for e in range(2, E):
                sp.wait_ge(expert_ready, max(2, e - 1))
                load_expert(e)
                sp.wait_ge(raw_loaded[e % 2], 48 * (e // 2 + 1))
                sp.sem_inc(raw_ready, 1)

        @block.gpsimd
        def _(pool):
            pool.memset(pad_rows[:], 0.0).then_inc(zeroed, 1)
            pool.memset(ident[:], 0.0).then_inc(zeroed, 1)
            pool.memset(before[:], 0.0).then_inc(zeroed, 1)
            pool.memset(ones[:], 1.0)
            pool.memset(kv[:], 0.0)
            pool.memset(counted[:], 0.0)
            pool.memset(minus_half[:], -0.5)
            pool.memset(v_aug[:], 1.0)
            pool.wait_ge(zeroed, 1)
            pool.iota(pad_rows[:, D:D + 1].bitcast(U32), pattern=[[0, 1]], base=T, channel_multiplier=1).then_inc(consts_ready, 1)
            pool.wait_ge(zeroed, 3)
            pool.affine_select(out=ident[:], in_=ident[:], compare_op=ALU.not_equal, fill=1.0, base=0,
                               pattern=[[-1, P]], channel_multiplier=1)
            pool.affine_select(out=before[:], in_=before[:], compare_op=ALU.is_ge, fill=1.0, base=0,
                               pattern=[[-1, P]], channel_multiplier=1)
            pool.iota(token_id[:], pattern=[[P, NT]], base=0, channel_multiplier=1)
            pool.iota(expert_no[:], pattern=[[1, E]], base=0, channel_multiplier=0, allow_small_or_imprecise_dtypes=True)
            pool.iota(expert_base[:], pattern=[[CAP, E]], base=0, channel_multiplier=0, allow_small_or_imprecise_dtypes=True)
            pool.iota(steps[:], pattern=[[0, E], [P, NT]], base=0, channel_multiplier=0, allow_small_or_imprecise_dtypes=True)
            pool.iota(tile_no[:], pattern=[[1, TILES], [0, E]], base=0, channel_multiplier=0,
                      allow_small_or_imprecise_dtypes=True).then_inc(consts_ready, 1)

            def inverse_root(r, var, half, step_sem, done):
                pool.tensor_scalar(r[0], var, EPS, None, ALU.add).then_inc(step_sem, 1)
                pool.wait_ge(step_sem, done + 1)
                pool.tensor_tensor(r[1], r[0], half, ALU.pow).then_inc(step_sem, 1)
                pool.wait_ge(step_sem, done + 2)
                pool.tensor_tensor(r[2], r[1], r[1], ALU.mult).then_inc(step_sem, 1)
                pool.wait_ge(step_sem, done + 3)
                pool.tensor_tensor(r[3], r[2], r[0], ALU.mult).then_inc(step_sem, 1)
                pool.wait_ge(step_sem, done + 4)
                settle(pool)
                pool.tensor_scalar(r[2], r[3], -0.5, 1.5, ALU.mult, ALU.add).then_inc(step_sem, 1)
                pool.wait_ge(step_sem, done + 5)
                pool.tensor_tensor(r[4], r[1], r[2], ALU.mult).then_inc(step_sem, 1)

            def inverse_roots(a, b, done):
                pool.wait_ge(mv_ready, b)
                settle(pool)
                inverse_root([rs1[:, i, a:b] for i in range(5)], mv[:, a:b, 1], minus_half[:, a:b], rs1_step, done)

            def low_piece(at, n):
                return pool.tensor_tensor(w_lo[:, bass.ds(at, n)], raw[:, bass.ds(at, n)],
                                          w_hi[:, bass.ds(at, n)].bitcast(F32), ALU.subtract)

            def step(s):
                if live(s, -3):
                    pool.wait_ge(rows_ready, s - 2)
                    pool.wait_ge(slot_ready, s - 2)
                    settle(pool)
                    for k in range(2):
                        pool.indirect_dma_start(out=bucket, out_offset=bass.IndirectOffsetOnAxis(ap=slot[:, k:k + 1], axis=0),
                                                in_=rows[:, k, :], in_offset=None).then_inc(scattered, 16)
                piece = piece_of(s)
                if piece is not None:
                    pool.wait_ge(hi_ready, s - 1)
                    last = low_piece(piece * PIECE, PIECE)
                    if isinstance(s, int) and s == NT - 3:
                        last.then_inc(expert_ready, 2)
                if live(s, -1):
                    pool.wait_ge(mv2_ready, s)
                    settle(pool)
                    inverse_root([rs2[:, i:i + 1] for i in range(5)], mv2[:, 1:2], minus_half[:, 0:1], rs2_step, 6 * (s - 1))
                if live(s, 0):
                    pool.tensor_tensor(xb[:], x_all[:, bass.ds(s * D, D)], bo_s[:], ALU.add).then_inc(xb_ready, 1)

            pool.wait_ge(consts_ready, 2)
            inverse_roots(0, 4, 0)
            pool.wait_ge(out_w_loaded, 48)
            steps_of_attention(pool, step, lambda: inverse_roots(4, NT, 6))

            pool.wait_ge(x2_stored, 16 * (NT + 1))
            pool.wait_ge(list_ready, 6)
            settle(pool)

            def add(t, v):
                pool.wait_ge(y_ready, t + 1)
                if tile_live(t, -1):
                    pool.wait_ge(y_added, 16 * t)
                settle(pool)
                pool.indirect_dma_start(out=out, out_offset=bass.IndirectOffsetOnAxis(ap=meta[:, v, 0:1].bitcast(U32), axis=0),
                                        in_=y[:, v, :], in_offset=None, compute_op=ALU.add).then_inc(y_added, 16)

            def mix(t, u):
                if not tile_live(t, -1):
                    return
                first = pool.value_load(tab_first[0:1, bass.ds(t, 1)], min_val=0, max_val=1)

                def low_halves(parts):
                    with pool.If(first):
                        e = pool.value_load(tab_expert[0:1, bass.ds(t, 1)], min_val=1, max_val=E - 2)
                        at = pool.snap(((e + 1) % 2) * WALL)
                        for i in parts:
                            pool.wait_ge(hi_ready, 3 * e + (NT - 6 + i))
                            last = low_piece(at + i * W13, W13)
                        if i == 2:
                            last.then_inc(expert_ready, 1)

                low_halves((0,))
                add(t - 1, (u - 1) % 4)
                low_halves((1, 2))

            rounds_of_mixture(pool, mix)
            n = tiles_used(pool)
            add(n - 1, 3)
            pool.wait_ge(y_added, 16 * n)

        @block.tensor
        def _(pe):
            def transposes(s):
                pe.wait_ge(xn_ready, s + 1)
                pe.wait_ge(c_loaded, 16 * (s + 1))
                for i, src in enumerate((xn, c_in)):
                    for k in range(KD):
                        last = nc.tensor.transpose(bank[4][:, (KD * i + k) * P:(KD * i + k + 1) * P],
                                                   src[:, k * P:(k + 1) * P], ident[:])
                last.then_inc(tr_done, 1)

            def project(b, w, at, done):
                for h in range(KD):
                    for k in range(KD):
                        last = nc.tensor.matmul(bank[b][:, h * P:(h + 1) * P], w[:, k, h * P:(h + 1) * P],
                                                xcT[:, at + k, :], start=(k == 0), stop=(k == KD - 1))
                last.then_inc(done, 1)

            def query_features(h):
                for j in range(HALF // P):
                    last = nc.tensor.matmul(bank[h][:, j * P:(j + 1) * P], bdq_s[:, j * P:(j + 1) * P],
                                            qT[:, h, :], start=True, stop=True)
                last.then_inc(qf_done, 1)

            def step(s):
                if live(s, 0):
                    pe.wait_ge(xcT_ready, s + 1)
                    if live(s, -1):
                        pe.wait_ge(qf_ready, 2 * s - 1)
                    project(0, wk_s, KD, k_done)
                if live(s, -2):
                    pe.wait_ge(xn2_ready, s - 1)
                    for k in range(KD):
                        last = nc.tensor.transpose(bank[7][:, k * P:(k + 1) * P], xn2[:, k * P:(k + 1) * P], ident[:])
                    last.then_inc(x2T_done, 1)
                if live(s, -1):
                    pe.wait_ge(qf_ready, 2 * s)
                    pe.wait_ge(kv_ready, 2 * s)
                    if live(s, -2):
                        pe.wait_ge(x2_ready, s - 1)
                    for j in range(PAIRS):
                        last = nc.tensor.matmul(bank[3][:, j * 2 * AUG:(j + 1) * 2 * AUG], qf[:, j * P:(j + 1) * P],
                                                kv[:, j, :], start=True, stop=True)
                    last.then_inc(qkv_done, 1)
                if live(s, 0):
                    project(1, wq_s, 0, q_done)
                if live(s, -2):
                    pe.wait_ge(x2T_ready, s - 1)
                    for k in range(KD):
                        last = nc.tensor.matmul(bank[7][:, 0:E], x2T[:, k, :], gate_s[:, k, :],
                                                start=(k == 0), stop=(k == KD - 1))
                    last.then_inc(logits_done, 1)
                if live(s, 0):
                    for k in range(KD):
                        last = nc.tensor.matmul(bank[2][:, 0:D], xcT[:, KD + k, :], wv_s[:, k, :],
                                                start=(k == 0), stop=(k == KD - 1))
                    last.then_inc(v_done, 1)
                if live(s, 1):
                    if live(s, -3):
                        pe.wait_ge(slot_ready, s - 2)
                    transposes(s + 1)
                if live(s, 0):
                    pe.wait_ge(kT_ready, s + 1)
                    for h in range(KD):
                        nc.tensor.matmul(bank[5 + h][:], kT[:, h, :], bdk_s[:], start=True, stop=True).then_inc(kf_done, 1)
                if live(s, -1):
                    pe.wait_ge(att_ready, s)
                    if live(s, -2):
                        pe.wait_ge(exp_ready, s - 1)
                    for k in range(KD):
                        last = nc.tensor.transpose(bank[7][:, k * P:(k + 1) * P],
                                                   att[:].rearrange("p h d -> p (h d)")[:, k * P:(k + 1) * P], ident[:])
                    last.then_inc(attT_done, 1)
                if live(s, 0):
                    pe.wait_ge(qT_ready, s + 1)
                    query_features(0)
                if live(s, -1):
                    pe.wait_ge(attT_ready, s)
                    for k in range(KD):
                        last = nc.tensor.matmul(bank[3][:, 0:D], attT[:, k, :], wo_s[:, k, :],
                                                start=(k == 0), stop=(k == KD - 1))
                    last.then_inc(proj_done, 1)
                if live(s, 0):
                    query_features(1)
                    pe.wait_ge(kf_ready, 2 * s + 2)
                    pe.wait_ge(v_ready, s + 1)
                    for j in range(PAIRS):
                        last = nc.tensor.matmul(bank[2][:, j * 2 * AUG:(j + 1) * 2 * AUG], kf[:, j * P:(j + 1) * P],
                                                v_aug[:, 2 * j:2 * j + 2, :], start=True, stop=True)
                    last.then_inc(kv_done, 1)
                if live(s, -2):
                    pe.wait_ge(chosen_ready, s - 1)
                    if live(s, -3):
                        pe.wait_ge(slot_ready, s - 2)
                    if live(s, 1):
                        pe.wait_ge(xcT_ready, s + 2)
                    nc.tensor.matmul(bank[4][:, 0:E], before[:], chosen[:], start=True, stop=False)
                    nc.tensor.matmul(bank[4][:, 0:E], ones[:], counted[:], start=False, stop=True).then_inc(rank_done, 1)

            pe.wait_ge(consts_ready, 2)
            transposes(0)
            pe.wait_ge(att_w_loaded, 144)
            pe.wait_ge(out_w_loaded, 48)
            steps_of_attention(pe, step)
            pe.wait_ge(slot_ready, NT)
            nc.tensor.matmul(bank[4][:, 0:E], ones[:], counted[:], start=True, stop=True).then_inc(counts_done, 1)
            pe.wait_ge(list_ready, 6)

            def x_transposes(t, u):
                pe.wait_ge(x_in_loaded[u], 16 * (t // 4 + 1))
                for k in range(KD):
                    last = nc.tensor.transpose(bank[7][:, k * P:(k + 1) * P], x_in[:, u, k * P:(k + 1) * P], ident[:])
                last.then_inc(xT_done, 1)

            def slot_at(t):
                e = pe.value_load(tab_expert[0:1, bass.ds(t, 1)], min_val=0, max_val=E - 1)
                return e, pe.snap((e % 2) * WALL)

            def hidden(t):
                e, at = slot_at(t)
                pe.wait_ge(x_lo_ready, t + 1)
                pe.wait_ge(expert_ready, e + 1)
                for c in range(2):
                    for k in range(KD):
                        for part, stationary in enumerate((x_hi, x_lo)):
                            for b, of in ((c, 0), (2 + c, W13)):
                                for w in ((w_hi, w_lo) if part == 0 else (w_hi,)):
                                    last = nc.tensor.matmul(bank[b][:, 0:MC], stationary[:, k, :],
                                                            w[:, bass.ds(at + (of + k * M + c * MC), MC)],
                                                            start=(k == 0 and part == 0 and w is w_hi),
                                                            stop=(k == KD - 1 and part == 1))
                    last.then_inc(h_done, 1)

            def output(t):
                _, at = slot_at(t)
                pe.wait_ge(g_lo_ready, t + 1)
                if tile_live(t, -1):
                    pe.wait_ge(y_ready, t)
                for k in range(MB):
                    for part, stationary in enumerate((g_hi, g_lo)):
                        for w in ((w_hi, w_lo) if part == 0 else (w_hi,)):
                            last = nc.tensor.matmul(bank[6][:, 0:D], stationary[:, k, :],
                                                    w[:, bass.ds(at + (2 * W13 + k * D), D)],
                                                    start=(k == 0 and part == 0 and w is w_hi),
                                                    stop=(k == MB - 1 and part == 1))
                last.then_inc(y_done, 1)

            def mix(t, u):
                hidden(t)
                x_transposes(t + 1, (u + 1) % 4)
                if tile_live(t, -1):
                    output(t - 1)
                for k in range(MB):
                    if k in (0, MC // P):
                        pe.wait_ge(g_ready, 2 * t + (1 if k == 0 else 2))
                    b, at = (4, k) if k < 4 else (5, k - 4)
                    last = nc.tensor.transpose(bank[b][:, at * P:(at + 1) * P], g[:, k * P:(k + 1) * P], ident[:])
                    if k in (3, MB - 1):
                        last.then_inc(gT_done, 1)

            x_transposes(0, 0)
            rounds_of_mixture(pe, mix)
            output(tiles_used(pe) - 1)

        @block.scalar
        def _(act):
            def evacuate_transposes(s):
                act.wait_ge(tr_done, s + 1)
                nc.scalar.copy(xcT[:].rearrange("p k n -> p (k n)"), bank[4][:]).then_inc(xcT_ready, 1)

            def add_bias(b, dst, bias, done, ready, s):
                act.wait_ge(done, s + 1)
                for h in range(KD):
                    last = nc.scalar.activation(dst[:, h, :], bank[b][:, h * P:(h + 1) * P], ACT.Identity,
                                                bias=bias[:, h:h + 1])
                last.then_inc(ready, 1)

            def step(s):
                if live(s, 0):
                    add_bias(0, kT, bk_s, k_done, kT_ready, s)
                if live(s, -2):
                    act.wait_ge(x2T_done, s - 1)
                    nc.scalar.copy(x2T[:].rearrange("p k n -> p (k n)"), bank[7][:, 0:D]).then_inc(x2T_ready, 1)
                if live(s, 0):
                    add_bias(1, qT, bq_s, q_done, qT_ready, s)
                if live(s, -2):
                    act.wait_ge(max_ready, s - 1)
                    nc.scalar.activation(ex[:], bank[7][:, 0:E], ACT.Exp, bias=neg_max[:],
                                         accum_out=ex_sum[:]).then_inc(exp_ready, 1)
                if live(s, 1):
                    evacuate_transposes(s + 1)
                if live(s, -1):
                    act.wait_ge(attT_done, s)
                    nc.scalar.copy(attT[:].rearrange("p k n -> p (k n)"), bank[7][:, 0:D]).then_inc(attT_ready, 1)
                if live(s, 0):
                    act.wait_ge(qf_done, 2 * s + 1)
                    nc.scalar.activation(qf[:, 0:HALF], bank[0][:], ACT.Relu).then_inc(qf_ready, 1)
                if live(s, -2):
                    if live(s, -3):
                        act.wait_ge(scattered, 32 * (s - 2))
                    nc.scalar.copy(rows[:, :, 0:D],
                                   xn2[:].rearrange("p (o d) -> p o d", o=1).to_broadcast([P, 2, D])).then_inc(rows_ready, 1)
                if live(s, 0):
                    act.wait_ge(qf_done, 2 * s + 2)
                    nc.scalar.activation(qf[:, HALF:2 * HALF], bank[1][:], ACT.Relu).then_inc(qf_ready, 1)
                    act.wait_ge(kv_done, s + 1)
                    for i in range(2):
                        lo = i * FD
                        src = bank[2][lo:lo + FD, 0:PAIRS * 2 * AUG].rearrange("p (j c) -> p j c", c=2 * AUG)
                        nc.scalar.copy(kv[lo:lo + FD, :, i * AUG:(i + 1) * AUG],
                                       src[:, :, i * AUG:(i + 1) * AUG]).then_inc(kv_ready, 1)

            evacuate_transposes(0)
            act.wait_ge(att_w_loaded, 144)
            act.wait_ge(consts_ready, 2)
            steps_of_attention(act, step)

            def load(t, u):
                at = act.value_load(tab_row[0:1, bass.ds(t, 1)], min_val=0, max_val=PAD_AT)
                if tile_live(t, -4):
                    act.wait_ge(meta_ready, t - 3)
                act.dma_start(x_in[:, u, :], bucket[bass.ds(at, P), :]).then_inc(x_in_loaded[u], 16)

            def evacuate_x(t):
                act.wait_ge(xT_done, t + 1)
                nc.scalar.copy(x_hi[:].rearrange("p k n -> p (k n)"), bank[7][:, 0:D]).then_inc(x_hi_ready, 1)

            def evacuate_y(t, v):
                act.wait_ge(y_done, t + 1)
                if tile_live(t, -4):
                    act.wait_ge(y_added, 16 * (t - 3))
                nc.scalar.activation(y[:, v, :], bank[6][:, 0:D], ACT.Copy, scale=meta[:, v, 1:2]).then_inc(y_ready, 1)

            def mix(t, u):
                if tile_live(t, -2):
                    load(t + 2, (u + 2) % 4)
                for c in range(2):
                    act.wait_ge(h_done, 2 * t + (c + 1))
                    nc.scalar.activation(silu[:, c, :], bank[c][:, 0:MC], ACT.Silu).then_inc(silu_ready, 1)
                evacuate_x(t + 1)
                if tile_live(t, -1):
                    evacuate_y(t - 1, (u - 1) % 4)
                for i, (b, n) in enumerate(((4, 4), (5, MB - 4))):
                    act.wait_ge(gT_done, 2 * t + (i + 1))
                    nc.scalar.copy(g_hi[:, 4 * i:4 * i + n, :].rearrange("p k n -> p (k n)"),
                                   bank[b][:, 0:n * P]).then_inc(g_hi_ready, 1)

            act.wait_ge(scattered, 32 * NT)
            act.wait_ge(pad0_stored, 16)
            act.wait_ge(list_ready, 6)
            load(0, 0)
            act.wait_ge(pads_stored, 16 * E)
            for t in range(1, 4):
                load(t, t)
            evacuate_x(0)
            rounds_of_mixture(act, mix)
            n = tiles_used(act)
            evacuate_y(n - 1, 3)
            act.wait_ge(x_in_loaded[1], 4 * n + 16)
            settle(act)

        @block.vector
        def _(dve):
            def statistics(a, b):
                for n in range(a, b):
                    if n % 4 == 0:
                        dve.wait_ge(x_loaded[n // 4], 16)
                    nc.vector.bn_stats(stats[:, n, :], x_all[:, n * D:(n + 1) * D]).then_inc(stats_ready, 1)
                for n in range(a, b):
                    dve.wait_ge(stats_ready, n + 1)
                    nc.vector.bn_aggr(mv[:, n, :], stats[:, n, :]).then_inc(mv_ready, 1)

            def normalise(s):
                nc.vector.tensor_scalar(xn[:], x_all[:, bass.ds(s * D, D)], mv[:, bass.ds(s, 1), 0:1].rearrange("p a b -> p (a b)"),
                                        rs1[:, 4, bass.ds(s, 1)], ALU.subtract, ALU.mult).then_inc(xn_ready, 1)

            def high_piece(at, n):
                nc.vector.tensor_copy(w_hi[:, bass.ds(at, n)], raw[:, bass.ds(at, n)]).then_inc(hi_ready, 1)

            statistics(0, 4)
            dve.wait_ge(rs1_step, 6)
            normalise(0)
            dve.wait_ge(tr_done, 1)
            normalise(1)
            dve.wait_ge(att_w_loaded, 144)
            dve.wait_ge(consts_ready, 2)

            def step(s):
                if live(s, -3):
                    n = 3 * (s - 3)
                    dve.wait_ge(rank_done, s - 2)
                    nc.vector.tensor_tensor(slot_of[:], bank[4][:, 0:E], expert_base[:], ALU.add).then_inc(slot_step, 1)
                    nc.vector.tensor_tensor(counted[:], counted[:], chosen[:], ALU.add)
                    dve.wait_ge(slot_step, n + 1)
                    nc.vector.tensor_tensor(picked[:], slot_of[:].rearrange("p (o e) -> p o e", o=1).to_broadcast([P, 2, E]),
                                            pick[:], ALU.mult).then_inc(slot_step, 1)
                    dve.wait_ge(slot_step, n + 2)
                    nc.vector.tensor_reduce(slot_f[:], picked[:], AX.X, ALU.add).then_inc(slot_step, 1)
                    dve.wait_ge(slot_step, n + 3)
                    nc.vector.tensor_copy(slot[:], slot_f[:]).then_inc(slot_ready, 1)
                if live(s, -1):
                    dve.wait_ge(qkv_done, s)
                    o = bank[3][:, 0:NH * AUG].rearrange("p (h c) -> p h c", c=AUG)
                    nc.vector.tensor_scalar(den[:].rearrange("p (h o) -> p h o", o=1), o[:, :, HD:AUG], 1e-8, None,
                                            ALU.add).then_inc(den_step, 1)
                    dve.wait_ge(den_step, 2 * s - 1)
                    nc.vector.reciprocal(rden[:], den[:]).then_inc(den_step, 1)
                    dve.wait_ge(den_step, 2 * s)
                    nc.vector.tensor_tensor(att[:], o[:, :, 0:HD], rden[:].rearrange("p (h o) -> p h o", o=1).to_broadcast([P, NH, HD]),
                                            ALU.mult).then_inc(att_ready, 1)
                if live(s, -2):
                    dve.wait_ge(logits_done, s - 1)
                    nc.vector.tensor_reduce(neg_max[:], bank[7][:, 0:E], AX.X, ALU.max, negate=True).then_inc(max_ready, 1)
                if live(s, 0):
                    dve.wait_ge(v_done, s + 1)
                    nc.vector.tensor_tensor(v_aug[:, :, 0:HD], bank[2][:, 0:D].rearrange("p (h d) -> p h d", d=HD),
                                            bv_s[:].rearrange("p (h d) -> p h d", d=HD), ALU.add).then_inc(v_ready, 1)
                if live(s, 2):
                    dve.wait_ge(tr_done, s + 2)
                    if isinstance(s, int) and s == 2:
                        dve.wait_ge(rs1_step, 12)
                    normalise(s + 2)
                piece = piece_of(s)
                if piece is not None:
                    if isinstance(s, int) and s == 2:
                        dve.wait_ge(raw_ready, 2)
                    high_piece(piece * PIECE, PIECE)
                if live(s, 0):
                    for h in range(KD):
                        dve.wait_ge(kf_done, 2 * s + (h + 1))
                        nc.vector.tensor_scalar(kf[:, h * HALF:(h + 1) * HALF], bank[5 + h][:], 0.0,
                                                mask_s[:, bass.ds(s, 1)], ALU.max, ALU.mult).then_inc(kf_ready, 1)
                if live(s, -2):
                    n = 8 * (s - 2)
                    dve.wait_ge(exp_ready, s - 1)
                    nc.vector.reciprocal(inv_sum[:], ex_sum[:]).then_inc(top_step, 1)
                    dve.wait_ge(top_step, n + 1)
                    nc.vector.tensor_scalar(prob[:], ex[:], inv_sum[:], None, ALU.mult).then_inc(top_step, 1)
                    dve.wait_ge(top_step, n + 2)
                    settle(dve)
                    nc.vector.max(best[:], prob[:]).then_inc(top_step, 1)
                    dve.wait_ge(top_step, n + 3)
                    settle(dve)
                    nc.vector.max_index(best_i[:], best[:], prob[:]).then_inc(top_step, 1)
                    nc.vector.tensor_tensor(top_sum[:], best[:, 0:1], best[:, 1:2], ALU.add).then_inc(top_step, 1)
                    dve.wait_ge(top_step, n + 4)
                    nc.vector.tensor_copy(best_f[:], best_i[:, 0:2]).then_inc(top_step, 1)
                    dve.wait_ge(top_step, n + 5)
                    nc.vector.reciprocal(inv_top[:], top_sum[:]).then_inc(top_step, 1)
                    dve.wait_ge(top_step, n + 6)
                    if live(s, -3):
                        dve.wait_ge(slot_ready, s - 2)
                        dve.wait_ge(scattered, 32 * (s - 2))
                    for k in range(2):
                        last = nc.vector.tensor_scalar(pick[:, k, :], expert_no[:], best_f[:, k:k + 1], None, ALU.is_equal)
                    last.then_inc(top_step, 1)
                    dve.wait_ge(top_step, n + 7)
                    nc.vector.tensor_scalar(rows[:, :, D + 1:D + 2].rearrange("p k o -> p (k o)"), best[:, 0:2], inv_top[:], None, ALU.mult)
                    nc.vector.tensor_copy(rows[:, :, D:D + 1].rearrange("p k o -> p (k o)").bitcast(U32),
                                          token_id[:, bass.ds(s - 2, 1)].to_broadcast([P, 2]))
                    dve.wait_ge(top_step, n + 8)
                    nc.vector.tensor_tensor(chosen[:], pick[:, 0, :], pick[:, 1, :], ALU.add).then_inc(chosen_ready, 1)
                if live(s, -1):
                    dve.wait_ge(proj_done, s)
                    dve.wait_ge(xb_ready, s)
                    if live(s, -2):
                        dve.wait_ge(x2_stored, 16 * s)
                    nc.vector.tensor_tensor(x2[:], bank[3][:, 0:D], xb[:], ALU.add).then_inc(x2_ready, 1)
                    dve.wait_ge(x2_ready, s)
                    nc.vector.bn_stats(stats2[:], x2[:]).then_inc(stats2_ready, 1)
                    dve.wait_ge(stats2_ready, s)
                    settle(dve)
                    nc.vector.bn_aggr(mv2[:], stats2[:]).then_inc(mv2_ready, 1)
                    dve.wait_ge(rs2_step, 6 * s)
                    if live(s, -2):
                        dve.wait_ge(rows_ready, s - 1)
                    nc.vector.tensor_scalar(xn2[:], x2[:], mv2[:, 0:1], rs2[:, 4:5],
                                            ALU.subtract, ALU.mult).then_inc(xn2_ready, 1)

            steps_of_attention(dve, step, lambda: statistics(4, NT))

            done = [0]

            def link(ins):
                done[0] += 1
                ins.then_inc(list_step, 1)
                dve.wait_ge(list_step, done[0])

            def wide(a):
                return a.rearrange("a (o e) -> a o e", o=1).to_broadcast([1, TILES, E])

            dve.wait_ge(counts_done, 1)
            link(nc.vector.tensor_copy(n_row[:], bank[4][0:1, 0:E]))
            nc.vector.tensor_copy(tab_count[:], n_row[:]).then_inc(list_ready, 1)
            link(nc.vector.tensor_tensor(more[:], n_row[:].rearrange("a (e o) -> a e o", o=1).to_broadcast([1, E, NT]),
                                         steps[:], ALU.is_gt))
            link(nc.vector.tensor_reduce(n_tiles[:], more[:], AX.X, ALU.add))
            link(nc.vector.tensor_scalar(ends[:, 0, :], n_tiles[:], 1.0, None, ALU.max))
            for i, by in enumerate((1, 2, 4)):
                link(nc.vector.tensor_copy(ends[:, i + 1, 0:by], ends[:, i, 0:by]))
                link(nc.vector.tensor_tensor(ends[:, i + 1, by:E], ends[:, i, by:E], ends[:, i, 0:E - by], ALU.add))
            link(nc.vector.tensor_scalar(active[:], tile_no[:, 0:4 * ROUNDS:4, 0], ends[:, 3, E - 1:E], None, ALU.is_lt))
            link(nc.vector.tensor_reduce(used[:, 0:1], active[:], AX.X, ALU.add))
            link(nc.vector.tensor_scalar(used[:, 1:2], used[:, 0:1], 4.0, -float(SURE), ALU.mult, ALU.add))
            nc.vector.tensor_copy(tab_active[:], active[:]).then_inc(list_ready, 1)
            nc.vector.tensor_copy(tab_used[:], used[:, 1:2]).then_inc(list_ready, 1)
            link(nc.vector.tensor_tensor(past[:], tile_no[:], wide(ends[:, 3, :]), ALU.is_ge))
            link(nc.vector.tensor_reduce(lists[:, 0, :], past[:], AX.X, ALU.add))
            link(nc.vector.tensor_scalar(lists[:, 1, :], lists[:, 0, :], float(E - 1), None, ALU.min))
            nc.vector.tensor_copy(tab_expert[:], lists[:, 1, :]).then_inc(list_ready, 1)
            link(nc.vector.tensor_scalar(n_tiles[:], ends[:, 0, :], -float(P), float(CAP), ALU.mult, ALU.add))
            link(nc.vector.tensor_tensor(skip[:], past[:], wide(n_tiles[:]), ALU.mult))
            link(nc.vector.tensor_reduce(lists[:, 2, :], skip[:], AX.X, ALU.add))
            link(nc.vector.scalar_tensor_tensor(out=lists[:, 3, :], in0=tile_no[:, :, 0], scalar=float(P),
                                                in1=lists[:, 2, :], op0=ALU.mult, op1=ALU.add))
            link(nc.vector.tensor_scalar(lists[:, 3, :], lists[:, 3, :], float(PAD_AT), None, ALU.min))
            nc.vector.tensor_copy(tab_row[:], lists[:, 3, :]).then_inc(list_ready, 1)
            link(nc.vector.memset(lists[:, 4, 0:1], 0.0))
            link(nc.vector.tensor_tensor(lists[:, 4, 1:TILES], lists[:, 1, 1:TILES], lists[:, 1, 0:TILES - 1], ALU.subtract))
            link(nc.vector.tensor_scalar(lists[:, 2, :], lists[:, 1, :], float(E - 1), None, ALU.is_lt))
            link(nc.vector.tensor_tensor(lists[:, 4, :], lists[:, 4, :], lists[:, 2, :], ALU.mult))
            nc.vector.tensor_copy(tab_first[:], lists[:, 4, :]).then_inc(list_ready, 1)
            dve.wait_ge(list_ready, 6)

            def split_x(t, u):
                dve.wait_ge(x_hi_ready, t + 1)
                nc.vector.tensor_tensor(x_lo[:].rearrange("p k n -> p (k n)"), bank[7][:, 0:D],
                                        x_hi[:].rearrange("p k n -> p (k n)").bitcast(F32), ALU.subtract).then_inc(x_lo_ready, 1)
                if tile_live(t, -4):
                    dve.wait_ge(y_added, 16 * (t - 3))
                nc.vector.tensor_copy(meta[:, u, :].bitcast(U32), x_in[:, u, D:ROW].bitcast(U32)).then_inc(meta_ready, 1)

            def mix(t, u):
                for c in range(2):
                    dve.wait_ge(silu_ready, 2 * t + (c + 1))
                    nc.vector.tensor_tensor(g[:, c * MC:(c + 1) * MC], bank[2 + c][:, 0:MC], silu[:, c, :],
                                            ALU.mult).then_inc(g_ready, 1)
                split_x(t + 1, (u + 1) % 4)
                for i, (b, n) in enumerate(((4, 4), (5, MB - 4))):
                    dve.wait_ge(g_hi_ready, 2 * t + (i + 1))
                    last = nc.vector.tensor_tensor(g_lo[:, 4 * i:4 * i + n, :].rearrange("p k n -> p (k n)"),
                                                   bank[b][:, 0:n * P],
                                                   g_hi[:, 4 * i:4 * i + n, :].rearrange("p k n -> p (k n)").bitcast(F32),
                                                   ALU.subtract)
                last.then_inc(g_lo_ready, 1)
                if tile_live(t, -1):
                    first = dve.value_load(tab_first[0:1, bass.ds(t, 1)], min_val=0, max_val=1)
                    with dve.If(first):
                        e = dve.value_load(tab_expert[0:1, bass.ds(t, 1)], min_val=1, max_val=E - 2)
                        dve.wait_ge(y_done, t)
                        dve.wait_ge(raw_ready, e + 2)
                        settle(dve)
                        at = dve.snap(((e + 1) % 2) * WALL)
                        for i in range(3):
                            high_piece(at + i * W13, W13)

            split_x(0, 0)
            rounds_of_mixture(dve, mix)


def kernel(**inputs):
    import numpy as np
    import concourse.bacc as bacc
    from concourse.bass_utils import run_bass_kernel_spmd as run

    def block_diagonal(w):
        wide = np.zeros((P, HALF), w.dtype)
        for h in range(P // HD):
            wide[h * HD:(h + 1) * HD, h * FD:(h + 1) * FD] = w.T
        return wide

    i = {k: np.asarray(v) for k, v in inputs.items()}
    a = {
        "x": i["x"].reshape(T, D), "ctx": i["ctx_2048"].reshape(T, D), "maskT": i["mask_BxS2_ff1"].T,
        "wqT": i["L0_xattn_Wq"].T, "bq": i["L0_xattn_bq"].reshape(KD, P).T,
        "wkT": i["L0_xattn_Wk"].T, "bk": i["L0_xattn_bk"].reshape(KD, P).T,
        "wvT": i["L0_xattn_Wv"].T, "bv": i["L0_xattn_bv"].reshape(1, D),
        "bdq": block_diagonal(i["L0_xattn_Wqf"]), "bdk": block_diagonal(i["L0_xattn_Wkf"]),
        "woT": i["L0_xattn_Wo"].T, "bo": i["L0_xattn_bo"].reshape(1, D),
        "gate": i["L0_ffn_gate_w"], "w1": i["L0_ffn_w1"], "w2": i["L0_ffn_w2"], "w3": i["L0_ffn_w3"],
    }
    a = {f"in_{k}": np.ascontiguousarray(v) for k, v in a.items()}
    nc = bacc.Bacc("TRN2", target_bir_lowering=False, num_devices=1)
    args = [nc.dram_tensor(k, v.shape, mybir.dt.from_np(v.dtype), kind="ExternalInput").ap() for k, v in a.items()]
    args.append(nc.dram_tensor("out_rows", (T + P, D), F32, kind="ExternalOutput").ap())
    build(nc, *args)
    r = run(nc, [a], core_ids=[0])
    return r.results[0]["out_rows"][0:T].reshape(NT, P, D)
```

```python
from contextlib import ExitStack

import concourse.bass as bass
from concourse import mybir

P = 128
T, D = 2048, 256
NT = T // P
KD = D // P
NH, HD, FD = 16, 16, 64
HALF = NH * FD // KD
PAIRS = NH // 2
AUG = HD + 1
E, M = 8, 896
MB = M // P
MC = M // 2
ROW = D + 2
CAP = T + P
PAD_AT = E * CAP
CUT = (0, 4, 8, 12, NT)
SURE = 2 * T // P
MOST = SURE + E
TILES = MOST + 2
W13, W2 = KD * M, MB * D
WALL = 2 * W13 + W2
PIECES = NT - 4
PIECE = 2 * WALL // PIECES
LATE = 3
EPS = 1e-5

F32 = mybir.dt.float32
F32R = mybir.dt.float32r
BF16 = mybir.dt.bfloat16
I32 = mybir.dt.int32
U32 = mybir.dt.uint32
ALU = mybir.AluOpType
ACT = mybir.ActivationFunctionType
AX = mybir.AxisListType


def build(nc, x, ctxT, maskT, wqT, bq, wkT, bk, wvT, bv, bdq, bdk, woT, bo, gate, w1, w2, w3, out):
    bucket = nc.dram_tensor("bucket", [PAD_AT + P, ROW], F32, kind="Internal").ap()

    with ExitStack() as stack:
        def sb(name, shape, dt=F32):
            return stack.enter_context(nc.sbuf_tensor(name, shape, dt))

        def sem(name):
            return stack.enter_context(nc.semaphore(name))

        bank = [stack.enter_context(nc.psum_tensor(f"bank{i}", [P, 512], F32)) for i in range(8)]

        raw = sb("raw", [P, 2 * WALL])
        w_hi = sb("w_hi", [P, 2 * WALL], F32R)
        w_lo = sb("w_lo", [P, 2 * WALL], F32R)
        ident = sb("ident", [P, P])
        ones = sb("ones", [P, P], BF16)
        before = sb("before", [P, P], BF16)
        expert_no = sb("expert_no", [P, E])
        expert_base = sb("expert_base", [P, E])
        token_id = sb("token_id", [P, NT], U32)
        minus_half = sb("minus_half", [P, NT])
        pad_rows = sb("pad_rows", [P, ROW])
        wq_s = sb("wq_s", [P, KD, D])
        staged = raw[:, WALL:WALL + 3 * KD * D + 2 * HALF]
        wk_s, wv_s, wo_s = (staged[:, i * KD * D:(i + 1) * KD * D].rearrange("p (k d) -> p k d", k=KD) for i in range(3))
        bdk_s, bdq_s = (staged[:, 3 * KD * D + i * HALF:3 * KD * D + (i + 1) * HALF] for i in range(2))
        wide_halves = sb("wide_halves", [P, 4, KD, D], F32R)
        wv_hi, wv_lo, wo_hi, wo_lo = (wide_halves[:, i] for i in range(4))
        wk_hi, wk_lo = sb("wk_hi", [P, KD, D], F32R), sb("wk_lo", [P, KD, D], F32R)
        bdk_hi, bdk_lo, bdq_hi, bdq_lo = (sb(n, [P, HALF], F32R) for n in ("bdk_hi", "bdk_lo", "bdq_hi", "bdq_lo"))
        bq_s, bk_s = sb("bq_s", [P, KD]), sb("bk_s", [P, KD])
        bv_s, bo_s = sb("bv_s", [P, D]), sb("bo_s", [P, D])
        gate_s = sb("gate_s", [P, KD, E])
        mask_s = sb("mask_s", [P, NT])
        x_all = sb("x_all", [P, NT * D])
        late = raw[:, 2 * WALL - LATE * D:2 * WALL]
        c_in = late[:, 0:KD * 2 * P].rearrange("p (k n) -> p k n", k=KD)
        xn = late[:, KD * 2 * P:KD * 2 * P + D]
        stats = sb("stats", [P, NT, 6])
        mv = sb("mv", [P, NT, 2])
        rs1 = sb("rs1", [P, 5, NT])
        xnT = sb("xnT", [P, KD, 2 * P])
        c_hi, c_lo, qT_hi, qT_lo, kT_hi, kT_lo = (sb(n, [P, KD, 2 * P], F32R)
                                                  for n in ("c_hi", "c_lo", "qT_hi", "qT_lo", "kT_hi", "kT_lo"))
        v_aug = sb("v_aug", [P, NH, AUG])
        qf, kf = sb("qf", [P, PAIRS, 2 * P]), sb("kf", [P, NH * FD])
        kv = sb("kv", [P, PAIRS, 2 * AUG])
        den = sb("den", [P, NH])
        rden = sb("rden", [P, NH])
        att = sb("att", [P, NH, HD])
        attT_hi, attT_lo = sb("attT_hi", [P, KD, P], F32R), sb("attT_lo", [P, KD, P], F32R)
        x2 = sb("x2", [P, D])
        stats2 = sb("stats2", [P, 6])
        mv2 = sb("mv2", [P, 2])
        rs2 = sb("rs2", [P, 5])
        xn2 = sb("xn2", [P, D])
        rows = sb("rows", [P, 2, ROW])
        x2T = sb("x2T", [P, KD, P])
        neg_max = sb("neg_max", [P, 1])
        ex = sb("ex", [P, E])
        silu_first = sb("silu_first", [P, 1])
        ex_sum = sb("ex_sum", [P, 1])
        inv_sum = sb("inv_sum", [P, 1])
        prob = sb("prob", [P, E])
        best = sb("best", [P, 8])
        best_i = sb("best_i", [P, 8], U32)
        best_f = sb("best_f", [P, 2])
        top_sum = sb("top_sum", [P, 1])
        inv_top = sb("inv_top", [P, 1])
        pick = sb("pick", [P, 2, E])
        chosen = sb("chosen", [P, E], BF16)
        counted = sb("counted", [P, E], BF16)
        slot_of = sb("slot_of", [P, E])
        picked = sb("picked", [P, 2, E])
        slot_f = sb("slot_f", [P, 2])
        slot = sb("slot", [P, 2], U32)
        steps = sb("steps", [1, E, NT])
        tile_no = sb("tile_no", [1, TILES])
        n_row = sb("n_row", [1, E])
        more = kf[0:1, 0:E * NT].rearrange("a (e n) -> a e n", e=E)
        lists = kf[0:1, E * NT:E * NT + 7 * TILES].rearrange("a (i t) -> a i t", i=7)
        n_tiles = sb("n_tiles", [1, E])
        ends = sb("ends", [1, 4, E])
        past, skip = (qf[0:1, 2 * i:2 * i + 2, :].rearrange("a j n -> a (j n)")[:, 0:TILES * E]
                      .rearrange("a (t e) -> a t e", e=E) for i in range(2))
        tab_count = sb("tab_count", [1, E], I32)
        used = sb("used", [1, 2])
        last_of = sb("last_of", [1, 4])
        tab_last = sb("tab_last", [1, 4], I32)
        tab_used = sb("tab_used", [1, 1], I32)
        active, is_last = lists[:, 5, :], lists[:, 6, 0:MOST]
        tab_row, tab_expert, tab_first, tab_active = (
            qf[0:1, 4, i * TILES:(i + 1) * TILES].bitcast(I32) for i in range(4))
        meta = sb("meta", [P, 4, 2])
        x_hi, x_lo = (a[:].rearrange("p k n -> p (k n)")[:, 0:D].rearrange("p (k n) -> p k n", n=P) for a in (c_hi, c_lo))
        halves = wide_halves[:].rearrange("p i k d -> p (i k d)")
        g_hi = halves[:, 0:M].rearrange("p (k n) -> p k n", n=P)
        g_lo = halves[:, M:2 * M].rearrange("p (k n) -> p k n", n=P)
        y = x_all[:, 0:4 * D].rearrange("p (u d) -> p u d", u=4)
        silu = x_all[:, 4 * D:4 * D + M].rearrange("p (c m) -> p c m", c=2)
        g = x_all[:, 4 * D + M:4 * D + 2 * M]
        last_rows = x_all[:, 0:2 * ROW].rearrange("p (k d) -> p k d", k=2)
        x_in = x_all[:, 4 * D + 2 * M:4 * D + 2 * M + 4 * ROW].rearrange("p (u d) -> p u d", u=4)

        x_loaded = [sem(f"x_loaded{i}") for i in range(4)]
        kv_w_loaded, att_w_loaded, out_w_loaded, c_loaded = sem("kv_w_loaded"), sem("att_w_loaded"), sem("out_w_loaded"), sem("c_loaded")
        att_halves, out_halves, c_hi_ready, c_lo_ready = sem("att_halves"), sem("out_halves"), sem("c_hi_ready"), sem("c_lo_ready")
        qT_lo_ready, kT_lo_ready, attT_lo_ready = sem("qT_lo_ready"), sem("kT_lo_ready"), sem("attT_lo_ready")
        raw_loaded = [sem("raw_loaded0"), sem("raw_loaded1")]
        raw_ready, hi_ready, expert_ready = sem("raw_ready"), sem("hi_ready"), sem("expert_ready")
        consts_ready, zeroed = sem("consts_ready"), sem("zeroed")
        stats_ready, mv_ready, rs1_step, xn_ready = sem("stats_ready"), sem("mv_ready"), sem("rs1_step"), sem("xn_ready")
        tr_done, xnT_ready = sem("tr_done"), sem("xnT_ready")
        k_done, q_done, v_done = sem("k_done"), sem("q_done"), sem("v_done")
        kT_ready, qT_ready, v_ready = sem("kT_ready"), sem("qT_ready"), sem("v_ready")
        kf_done, qf_done, kf_ready, qf_ready = sem("kf_done"), sem("qf_done"), sem("kf_ready"), sem("qf_ready")
        kv_done, kv_ready, qkv_done = sem("kv_done"), sem("kv_ready"), sem("qkv_done")
        den_step, att_ready = sem("den_step"), sem("att_ready")
        attT_done, attT_ready, proj_done = sem("attT_done"), sem("attT_ready"), sem("proj_done")
        xb_ready, x2_ready, x2_stored = sem("xb_ready"), sem("x2_ready"), sem("x2_stored")
        stats2_ready, mv2_ready, rs2_step = sem("stats2_ready"), sem("mv2_ready"), sem("rs2_step")
        xn2_ready, rows_ready = sem("xn2_ready"), sem("rows_ready")
        x2T_done, x2T_ready, logits_done = sem("x2T_done"), sem("x2T_ready"), sem("logits_done")
        max_ready, exp_ready, top_step, chosen_ready = sem("max_ready"), sem("exp_ready"), sem("top_step"), sem("chosen_ready")
        rank_done, slot_step, slot_ready, scattered = sem("rank_done"), sem("slot_step"), sem("slot_ready"), sem("scattered")
        counts_done, list_step, list_ready = sem("counts_done"), sem("list_step"), sem("list_ready")
        late_loaded = sem("late_loaded")
        pad_stored = [sem(f"pad_stored{i}") for i in range(3)]
        gate_pass = sem("gate_pass")
        x_in_loaded = [sem(f"x_in_loaded{i}") for i in range(4)]
        xT_done, x_hi_ready, x_lo_ready = sem("xT_done"), sem("x_hi_ready"), sem("x_lo_ready")
        h_done, silu_ready, g_ready = sem("h_done"), sem("silu_ready"), sem("g_ready")
        gT_done, g_hi_ready, g_lo_ready = sem("gT_done"), sem("g_hi_ready"), sem("g_lo_ready")
        y_done, y_ready, y_added, meta_ready = sem("y_done"), sem("y_ready"), sem("y_added"), sem("meta_ready")

        def settle(eng):
            eng.sem_inc(gate_pass, 1)

        def steps_of_attention(step, eng, behind_first=None):
            for s in range(4):
                step(s, s // 2, s % 2)
                if s < 3 and behind_first:
                    behind_first(s)
            with eng.Fori(2, NT // 2 - 2) as p:
                for odd in range(2):
                    step(2 * p + odd, p, odd)
            for s in range(NT - 4, NT + 3):
                step(s, s // 2, s % 2)

        def live(s, ahead):
            return not isinstance(s, int) or 0 <= s + ahead < NT

        def behind(s):
            return isinstance(s, int) and s == NT

        def read_bank(s):
            return bank[0 if behind(s) else 3]

        def rows_of(t):
            return last_rows if isinstance(t, int) and t == NT - 1 else rows

        def piece_of(s):
            if not isinstance(s, int) or 2 <= s < NT - 3:
                return s - 2
            return PIECES - 1 if s == NT - 1 else None

        def tiles_of_mixture(eng, step):
            for t in range(8):
                step(t, t % 4)
            with eng.Fori(1, SURE // 8) as r:
                for i in range(8):
                    step(8 * r + i, i % 4)
            with eng.Fori(SURE // 4, MOST // 4) as r:
                def tile_if_used(i):
                    go = eng.value_load(tab_active[0:1, bass.ds(4 * r + i, 1)], min_val=0, max_val=1)
                    with eng.If(go):
                        step(4 * r + i, i)
                        if i < 3:
                            tile_if_used(i + 1)

                tile_if_used(0)

        def last_tile(eng, drain):
            n = tiles_used(eng)
            for v in range(4):
                with eng.If(eng.value_load(tab_last[0:1, v:v + 1], min_val=0, max_val=1)):
                    drain(n, v)
            return n

        def tile_live(t, ahead):
            return not isinstance(t, int) or t + ahead >= 0

        def tiles_used(eng):
            return eng.value_load(tab_used[0:1, 0:1], min_val=0, max_val=MOST - SURE) + SURE

        def weight_rows(e):
            return (
                (0, W13, w1[e].rearrange("(k p) m -> p k m", p=P), M),
                (W13, W13, w3[e].rearrange("(k p) m -> p k m", p=P), M),
                (2 * W13, W2, w2[e].rearrange("(k p) m -> p k m", p=P), D),
            )

        def context(p):
            return ctxT.rearrange("(k p) t -> p k t", p=P)[:, :, bass.ds(p * (2 * P), 2 * P)]

        block = stack.enter_context(nc.Block())

        @block.sync
        def _(sp):
            def load_expert(e, held_back=0):
                for i, (at, n, src, width) in enumerate(weight_rows(e)):
                    if i == 2 and held_back:
                        src, n = src[:, 0:MB - held_back, :], n - held_back * D
                    dst = raw[:, (e % 2) * WALL + at:(e % 2) * WALL + at + n]
                    sp.dma_start(dst.rearrange("p (k m) -> p k m", m=width), src).then_inc(raw_loaded[e % 2], 16)

            for i, (a, b) in enumerate(zip(CUT, CUT[1:])):
                src = x[a * P:b * P, :].rearrange("(n p) d -> p n d", p=P)
                sp.dma_start(x_all[:, a * D:b * D].rearrange("p (n d) -> p n d", d=D), src).then_inc(x_loaded[i], 16)
                if i == 0:
                    sp.dma_start(c_in, context(0)).then_inc(c_loaded, 16)
                    sp.dma_start(bdk_s, bdk).then_inc(att_w_loaded, 16)
                    sp.dma_start(wq_s[:], wqT.rearrange("(k p) n -> p k n", p=P)).then_inc(att_w_loaded, 16)
                    sp.dma_start(bdq_s, bdq).then_inc(att_w_loaded, 16)
                    sp.dma_start(wo_s, woT.rearrange("(k p) n -> p k n", p=P)).then_inc(out_w_loaded, 16)
                    sp.dma_start(gate_s[:], gate.rearrange("(k p) n -> p k n", p=P)).then_inc(out_w_loaded, 16)
                    sp.dma_start(bo_s[:], bo.to_broadcast([P, D])).then_inc(out_w_loaded, 16)
            sp.wait_ge(consts_ready, 1)
            sp.dma_start(out[T:T + P, :], pad_rows[:, 0:D]).then_inc(x2_stored, 16)
            sp.dma_start(bucket[PAD_AT:PAD_AT + P, :], pad_rows[:]).then_inc(pad_stored[1], 16)

            def step(s, p, odd):
                if not odd and live(s, 2):
                    sp.wait_ge(c_lo_ready, p + 1)
                    sp.dma_start(c_in, context(p + 1)).then_inc(c_loaded, 16)
                if isinstance(s, int) and 0 < s < 3:
                    sp.wait_ge(c_loaded, 16 * (s + 1))
                    if s == 1:
                        load_expert(0)
                    else:
                        sp.wait_ge(att_halves, 8)
                        sp.wait_ge(out_halves, 2)
                        load_expert(1, held_back=LATE)
                if isinstance(s, int) and s == NT - 2:
                    sp.wait_ge(tr_done, NT)
                    sp.wait_ge(c_lo_ready, NT // 2)
                    sp.dma_start(late.rearrange("p (k m) -> p k m", m=D),
                                 w2[1].rearrange("(k p) m -> p k m", p=P)[:, MB - LATE:MB, :]).then_inc(late_loaded, 16)
                if live(s, -1):
                    sp.wait_ge(x2_ready, s)
                    sp.dma_start(out[bass.ds((s - 1) * P, P), :], x2[:]).then_inc(x2_stored, 16)

            steps_of_attention(step, sp)
            sp.wait_ge(list_ready, 1)
            for e in range(E):
                n = sp.value_load(tab_count[0:1, e:e + 1], min_val=0, max_val=T)
                done = pad_stored[0 if e == 0 else 1 if e < 4 else 2]
                sp.dma_start(bucket[bass.ds(n + e * CAP, P), :], pad_rows[:]).then_inc(done, 16)
                if e == 0:
                    sp.wait_ge(x_in_loaded[0], 16)
            for e in range(2, E):
                sp.wait_ge(expert_ready, max(2, e - 1))
                load_expert(e)
                sp.wait_ge(raw_loaded[e % 2], 48 * (e // 2 + 1))
                sp.sem_inc(raw_ready, 1)

        @block.gpsimd
        def _(pool):
            pool.memset(pad_rows[:], 0.0).then_inc(zeroed, 1)
            pool.memset(ident[:], 0.0).then_inc(zeroed, 1)
            pool.memset(before[:], 0.0).then_inc(zeroed, 1)
            pool.memset(ones[:], 1.0)
            pool.memset(kv[:], 0.0)
            pool.memset(counted[:], 0.0)
            pool.memset(minus_half[:], -0.5)
            pool.memset(v_aug[:], 1.0)
            pool.wait_ge(zeroed, 1)
            pool.iota(pad_rows[:, D:D + 1].bitcast(U32), pattern=[[0, 1]], base=T, channel_multiplier=1).then_inc(consts_ready, 1)
            pool.wait_ge(zeroed, 3)
            pool.affine_select(out=ident[:], in_=ident[:], compare_op=ALU.not_equal, fill=1.0, base=0,
                               pattern=[[-1, P]], channel_multiplier=1)
            pool.affine_select(out=before[:], in_=before[:], compare_op=ALU.is_ge, fill=1.0, base=0,
                               pattern=[[-1, P]], channel_multiplier=1)
            pool.iota(token_id[:], pattern=[[P, NT]], base=0, channel_multiplier=1)
            pool.iota(expert_no[:], pattern=[[1, E]], base=0, channel_multiplier=0, allow_small_or_imprecise_dtypes=True)
            pool.iota(expert_base[:], pattern=[[CAP, E]], base=0, channel_multiplier=0, allow_small_or_imprecise_dtypes=True)
            pool.iota(steps[:], pattern=[[0, E], [P, NT]], base=0, channel_multiplier=0, allow_small_or_imprecise_dtypes=True)
            pool.iota(tile_no[:], pattern=[[1, TILES]], base=0, channel_multiplier=0,
                      allow_small_or_imprecise_dtypes=True).then_inc(consts_ready, 1)

            def inverse_root(r, var, half, step_sem, done):
                pool.tensor_scalar(r[0], var, EPS, None, ALU.add).then_inc(step_sem, 1)
                pool.wait_ge(step_sem, done + 1)
                pool.tensor_tensor(r[1], r[0], half, ALU.pow).then_inc(step_sem, 1)
                pool.wait_ge(step_sem, done + 2)
                pool.tensor_tensor(r[2], r[1], r[1], ALU.mult).then_inc(step_sem, 1)
                pool.wait_ge(step_sem, done + 3)
                pool.tensor_tensor(r[3], r[2], r[0], ALU.mult).then_inc(step_sem, 1)
                pool.wait_ge(step_sem, done + 4)
                settle(pool)
                pool.tensor_scalar(r[2], r[3], -0.5, 1.5, ALU.mult, ALU.add).then_inc(step_sem, 1)
                pool.wait_ge(step_sem, done + 5)
                pool.tensor_tensor(r[4], r[1], r[2], ALU.mult).then_inc(step_sem, 1)

            def inverse_roots(a, b, done):
                pool.wait_ge(mv_ready, b)
                settle(pool)
                inverse_root([rs1[:, i, a:b] for i in range(5)], mv[:, a:b, 1], minus_half[:, a:b], rs1_step, done)

            def low_piece(at, n):
                return pool.tensor_tensor(w_lo[:, bass.ds(at, n)], raw[:, bass.ds(at, n)],
                                          w_hi[:, bass.ds(at, n)].bitcast(F32), ALU.subtract)

            def low_context(p):
                pool.wait_ge(c_hi_ready, p + 1)
                pool.tensor_tensor(c_lo[:], c_in, c_hi[:].bitcast(F32), ALU.subtract).then_inc(c_lo_ready, 1)

            def step(s, p, odd):
                if odd and live(s, 1):
                    low_context(p + 1)
                if live(s, -3):
                    pool.wait_ge(rows_ready, s - 2)
                    pool.wait_ge(slot_ready, s - 2)
                    settle(pool)
                    for k in range(2):
                        pool.indirect_dma_start(out=bucket, out_offset=bass.IndirectOffsetOnAxis(ap=slot[:, k:k + 1], axis=0),
                                                in_=rows_of(s - 3)[:, k, :], in_offset=None).then_inc(scattered, 16)
                piece = piece_of(s)
                if piece is not None:
                    pool.wait_ge(hi_ready, piece + 1)
                    last = low_piece(piece * PIECE, PIECE)
                    if isinstance(s, int) and s == NT - 1:
                        last.then_inc(expert_ready, 2)
                if live(s, -1):
                    pool.wait_ge(mv2_ready, s)
                    settle(pool)
                    inverse_root([rs2[:, i:i + 1] for i in range(5)], mv2[:, 1:2], minus_half[:, 0:1], rs2_step, 6 * (s - 1))
                if live(s, 0):
                    if isinstance(s, int) and s == 0:
                        pool.wait_ge(out_w_loaded, 48)
                    pool.wait_ge(xn_ready, s + 1)
                    pool.tensor_tensor(x_all[:, bass.ds(s * D, D)], x_all[:, bass.ds(s * D, D)], bo_s[:], ALU.add).then_inc(xb_ready, 1)

            pool.wait_ge(consts_ready, 2)
            inverse_roots(0, CUT[1], 0)
            low_context(0)
            steps_of_attention(step, pool, lambda s: inverse_roots(CUT[s + 1], CUT[s + 2], 6 * s + 6))

            pool.wait_ge(x2_stored, 16 * (NT + 1))
            pool.wait_ge(list_ready, 7)
            settle(pool)

            def add(t, v):
                pool.wait_ge(y_ready, t + 1)
                if tile_live(t, -1):
                    pool.wait_ge(y_added, 16 * t)
                settle(pool)
                pool.indirect_dma_start(out=out, out_offset=bass.IndirectOffsetOnAxis(ap=meta[:, v, 0:1].bitcast(U32), axis=0),
                                        in_=y[:, v, :], in_offset=None, compute_op=ALU.add).then_inc(y_added, 16)

            def mix(t, u):
                if not tile_live(t, -1):
                    return
                first = pool.value_load(tab_first[0:1, bass.ds(t, 1)], min_val=0, max_val=1)

                def low_halves(parts):
                    with pool.If(first):
                        e = pool.value_load(tab_expert[0:1, bass.ds(t, 1)], min_val=1, max_val=E - 2)
                        at = pool.snap(((e + 1) % 2) * WALL)
                        for i in parts:
                            pool.wait_ge(hi_ready, 3 * e + (PIECES - 2 + i))
                            last = low_piece(at + i * W13, W13)
                        if i == 2:
                            last.then_inc(expert_ready, 1)

                low_halves((0,))
                add(t - 1, (u - 1) % 4)
                low_halves((1, 2))

            tiles_of_mixture(pool, mix)
            n = last_tile(pool, lambda n, v: add(n - 1, v))
            pool.wait_ge(y_added, 16 * n)

        @block.tensor
        def _(pe):
            def transposes(s):
                pe.wait_ge(xn_ready, s + 1)
                for k in range(KD):
                    last = nc.tensor.transpose(bank[4][:, k * P:(k + 1) * P], xn[:, k * P:(k + 1) * P], ident[:])
                last.then_inc(tr_done, 1)

            def project_queries(p):
                for h in range(KD):
                    for k in range(KD):
                        last = nc.tensor.matmul(bank[1][:, h * 2 * P:(h + 1) * 2 * P], wq_s[:, k, h * P:(h + 1) * P],
                                                xnT[:, k, :], start=(k == 0), stop=(k == KD - 1))
                last.then_inc(q_done, 1)

            def project_keys(p):
                pe.wait_ge(c_lo_ready, p + 1)
                for h in range(KD):
                    for k in range(KD):
                        last = halves_product(bank[0][:, h * 2 * P:(h + 1) * 2 * P],
                                              (wk_hi[:, k, h * P:(h + 1) * P], wk_lo[:, k, h * P:(h + 1) * P]),
                                              (c_hi[:, k, :], c_lo[:, k, :]), k == 0, k == KD - 1)
                last.then_inc(k_done, 1)

            def query_features(h):
                for i in range(2):
                    for j in range(2):
                        at = (2 * i + j) * P
                        last = halves_product(bank[i][:, j * 2 * P:(j + 1) * 2 * P],
                                              (bdq_hi[:, at:at + P], bdq_lo[:, at:at + P]),
                                              (qT_hi[:, h, :], qT_lo[:, h, :]), True, True)
                    last.then_inc(qf_done, 1)

            def halves_product(out_ap, lhs, rhs, start, stop):
                (a_hi, a_lo), (b_hi, b_lo) = lhs, rhs
                nc.tensor.matmul(out_ap, a_hi, b_hi, start=start, stop=False)
                nc.tensor.matmul(out_ap, a_hi, b_lo, start=False, stop=False)
                return nc.tensor.matmul(out_ap, a_lo, b_hi, start=False, stop=stop)

            def read(s, odd, js):
                for j in js:
                    last = nc.tensor.matmul(read_bank(s)[:, j * 2 * AUG:(j + 1) * 2 * AUG],
                                            qf[:, j, (1 - odd) * P:(2 - odd) * P],
                                            kv[:, j, :], start=True, stop=True)
                return last

            def gather(s, js):
                for j in js:
                    last = nc.tensor.matmul(bank[2][:, j * 2 * AUG:(j + 1) * 2 * AUG], kf[:, j * P:(j + 1) * P],
                                            v_aug[:, 2 * j:2 * j + 2, :], start=True, stop=True)
                return last

            def key_features(odd, h):
                tile = slice(odd * P, (odd + 1) * P)
                halves_product(bank[5 + h][:], (kT_hi[:, h, tile], kT_lo[:, h, tile]), (bdk_hi[:], bdk_lo[:]),
                               True, True).then_inc(kf_done, 1)

            def transpose_attention(s):
                pe.wait_ge(att_ready, s)
                for k in range(KD):
                    last = nc.tensor.transpose(bank[5][:, k * P:(k + 1) * P],
                                               att[:].rearrange("p h d -> p (h d)")[:, k * P:(k + 1) * P], ident[:])
                last.then_inc(attT_done, 1)

            def project_attention(s):
                pe.wait_ge(attT_lo_ready, s)
                if isinstance(s, int) and s == 1:
                    pe.wait_ge(out_w_loaded, 48)
                    pe.wait_ge(out_halves, 2)
                if behind(s):
                    pe.wait_ge(x2_ready, s - 1)
                for k in range(KD):
                    last = halves_product(bank[3][:, 0:D], (attT_hi[:, k, :], attT_lo[:, k, :]),
                                          (wo_hi[:, k, :], wo_lo[:, k, :]), k == 0, k == KD - 1)
                last.then_inc(proj_done, 1)

            def step(s, p, odd):
                if live(s, 0):
                    if isinstance(s, int) and s == 0:
                        pe.wait_ge(att_halves, 4)
                    tile = slice(odd * P, (odd + 1) * P)
                    for k in range(KD):
                        last = halves_product(bank[6][:, 0:D], (c_hi[:, k, tile], c_lo[:, k, tile]),
                                              (wv_hi[:, k, :], wv_lo[:, k, :]), k == 0, k == KD - 1)
                    last.then_inc(v_done, 1)
                if live(s, 0) and not odd:
                    pe.wait_ge(xnT_ready, s + 2)
                    if isinstance(s, int) and s == 0:
                        pe.wait_ge(att_w_loaded, 80)
                    if live(s, -1):
                        pe.wait_ge(qf_ready, 4 * p)
                    project_queries(p)
                if live(s, 0) and odd:
                    pe.wait_ge(qf_ready, 4 * p + 2)
                    query_features(1)
                if live(s, -1):
                    if behind(s):
                        pe.wait_ge(qf_ready, 4 * p)
                    pe.wait_ge(kv_ready, 2 * s)
                    if live(s, -2) and not behind(s):
                        pe.wait_ge(x2_ready, s - 1)
                    read(s, odd, range(PAIRS // 2))
                    if behind(s):
                        read(s, odd, range(PAIRS // 2, PAIRS)).then_inc(qkv_done, 1)
                if live(s, -3):
                    pe.wait_ge(chosen_ready, s - 2)
                    if live(s, 1) and odd:
                        pe.wait_ge(xnT_ready, s + 2)
                    if live(s, -4) and not live(s, 1):
                        pe.wait_ge(slot_ready, s - 3)
                    nc.tensor.matmul(bank[4][:, 0:E], before[:], chosen[:], start=True, stop=False)
                    nc.tensor.matmul(bank[4][:, 0:E], ones[:], counted[:], start=False, stop=True).then_inc(rank_done, 1)
                if live(s, 0):
                    if not odd:
                        pe.wait_ge(kT_lo_ready, p + 1)
                    if isinstance(s, int) and s == 0:
                        pe.wait_ge(att_halves, 6)
                    key_features(odd, 0)
                    pe.wait_ge(v_ready, s + 1)
                    key_features(odd, 1)
                if behind(s):
                    transpose_attention(s)
                if live(s, -2):
                    pe.wait_ge(xn2_ready, s - 1)
                    if live(s, -3):
                        pe.wait_ge(exp_ready, s - 2)
                    for k in range(KD):
                        last = nc.tensor.transpose(bank[7][:, k * P:(k + 1) * P], xn2[:, k * P:(k + 1) * P], ident[:])
                    last.then_inc(x2T_done, 1)
                if live(s, 2):
                    if live(s, -3):
                        pe.wait_ge(slot_ready, s - 2)
                    elif odd:
                        pe.wait_ge(xnT_ready, s + 2)
                    transposes(s + 2)
                if behind(s):
                    project_attention(s)
                if live(s, -1) and not behind(s):
                    if odd:
                        pe.wait_ge(qf_ready, 4 * p + 4)
                    read(s, odd, range(PAIRS // 2, PAIRS)).then_inc(qkv_done, 1)
                if live(s, -2):
                    pe.wait_ge(x2T_ready, s - 1)
                    for k in range(KD):
                        last = nc.tensor.matmul(bank[7][:, 0:E], x2T[:, k, :], gate_s[:, k, :],
                                                start=(k == 0), stop=(k == KD - 1))
                    last.then_inc(logits_done, 1)
                if live(s, 0) and not odd:
                    pe.wait_ge(qT_lo_ready, p + 1)
                    if isinstance(s, int) and s == 0:
                        pe.wait_ge(att_halves, 8)
                    query_features(0)
                if odd and live(s, 1):
                    project_keys(p + 1)
                if live(s, 0):
                    pe.wait_ge(kf_ready, 2 * s + 1)
                    gather(s, range(2))
                if live(s, -1) and not behind(s):
                    transpose_attention(s)
                if live(s, 0):
                    pe.wait_ge(kf_ready, 2 * s + 2)
                    gather(s, range(2, PAIRS)).then_inc(kv_done, 1)
                if live(s, -1) and not behind(s):
                    project_attention(s)

            pe.wait_ge(consts_ready, 2)
            transposes(0)
            pe.wait_ge(xnT_ready, 1)
            transposes(1)
            pe.wait_ge(att_halves, 2)
            project_keys(0)
            steps_of_attention(step, pe)
            pe.wait_ge(slot_ready, NT)
            nc.tensor.matmul(bank[4][:, 0:E], ones[:], counted[:], start=True, stop=True).then_inc(counts_done, 1)

            def x_transposes(t, u):
                pe.wait_ge(x_in_loaded[u], 16 * (t // 4 + 1))
                for k in range(KD):
                    last = nc.tensor.transpose(bank[7][:, k * P:(k + 1) * P], x_in[:, u, k * P:(k + 1) * P], ident[:])
                last.then_inc(xT_done, 1)

            def slot_at(t):
                if isinstance(t, int) and t == 0:
                    return 0, 0
                e = pe.value_load(tab_expert[0:1, bass.ds(t, 1)], min_val=0, max_val=E - 1)
                return e, pe.snap((e % 2) * WALL)

            def hidden(t):
                e, at = slot_at(t)
                pe.wait_ge(x_lo_ready, t + 1)
                pe.wait_ge(expert_ready, e + 1)
                for c in range(2):
                    for k in range(KD):
                        for part, stationary in enumerate((x_hi, x_lo)):
                            for b, of in ((c, 0), (2 + c, W13)):
                                for w in ((w_hi, w_lo) if part == 0 else (w_hi,)):
                                    last = nc.tensor.matmul(bank[b][:, 0:MC], stationary[:, k, :],
                                                            w[:, bass.ds(at + (of + k * M + c * MC), MC)],
                                                            start=(k == 0 and part == 0 and w is w_hi),
                                                            stop=(k == KD - 1 and part == 1))
                    last.then_inc(h_done, 1)

            def output(t):
                _, at = slot_at(t)
                pe.wait_ge(g_lo_ready, t + 1)
                if tile_live(t, -1):
                    pe.wait_ge(y_ready, t)
                for k in range(MB):
                    for part, stationary in enumerate((g_hi, g_lo)):
                        for w in ((w_hi, w_lo) if part == 0 else (w_hi,)):
                            last = nc.tensor.matmul(bank[6][:, 0:D], stationary[:, k, :],
                                                    w[:, bass.ds(at + (2 * W13 + k * D), D)],
                                                    start=(k == 0 and part == 0 and w is w_hi),
                                                    stop=(k == MB - 1 and part == 1))
                last.then_inc(y_done, 1)

            def mix(t, u):
                hidden(t)
                x_transposes(t + 1, (u + 1) % 4)
                if isinstance(t, int) and t == 0:
                    pe.wait_ge(list_ready, 7)
                if tile_live(t, -1):
                    output(t - 1)
                for k in range(MB):
                    if k in (0, MC // P):
                        pe.wait_ge(g_ready, 2 * t + (1 if k == 0 else 2))
                    b, at = (4, k) if k < 4 else (5, k - 4)
                    last = nc.tensor.transpose(bank[b][:, at * P:(at + 1) * P], g[:, k * P:(k + 1) * P], ident[:])
                    if k in (3, MB - 1):
                        last.then_inc(gT_done, 1)

            x_transposes(0, 0)
            tiles_of_mixture(pe, mix)
            output(tiles_used(pe) - 1)

        @block.scalar
        def _(act):
            def evacuate_transposes(s, odd):
                act.wait_ge(tr_done, s + 1)
                nc.scalar.copy(xnT[:, :, odd * P:(odd + 1) * P],
                               bank[4][:, 0:D].rearrange("p (k n) -> p k n", n=P)).then_inc(xnT_ready, 1)

            def high_context(p):
                act.wait_ge(c_loaded, 16 * (p + 1))
                nc.scalar.copy(c_hi[:], c_in).then_inc(c_hi_ready, 1)

            def add_bias(b, dst, bias, done, ready, p):
                act.wait_ge(done, p + 1)
                for h in range(KD):
                    last = nc.scalar.activation(dst[:, h, :], bank[b][:, h * 2 * P:(h + 1) * 2 * P], ACT.Identity,
                                                bias=bias[:, h:h + 1])
                last.then_inc(ready, 1)

            def query_features(p, h):
                for i in range(2):
                    act.wait_ge(qf_done, 4 * p + (2 * h + i + 1))
                    nc.scalar.activation(qf[:, 4 * h + 2 * i:4 * h + 2 * i + 2, :].rearrange("p j n -> p (j n)"), bank[i][:],
                                         ACT.Relu).then_inc(qf_ready, 1)

            def high_attention(s):
                act.wait_ge(attT_done, s)
                nc.scalar.copy(attT_hi[:].rearrange("p k n -> p (k n)"), bank[5][:, 0:D]).then_inc(attT_ready, 1)

            def step(s, p, odd):
                if odd and live(s, 1):
                    act.wait_ge(v_done, s + 1)
                    high_context(p + 1)
                if live(s, 0) and not odd:
                    add_bias(1, qT_hi, bq_s, q_done, qT_ready, p)
                if live(s, 0) and odd:
                    query_features(p, 1)
                piece = piece_of(s)
                if piece is not None:
                    act.wait_ge(raw_loaded[0 if isinstance(s, int) and s == 2 else 1], 48)
                    if isinstance(s, int) and s == NT - 1:
                        act.wait_ge(late_loaded, 16)
                    nc.scalar.copy(w_hi[:, bass.ds(piece * PIECE, PIECE)],
                                   raw[:, bass.ds(piece * PIECE, PIECE)]).then_inc(hi_ready, 1)
                if behind(s):
                    high_attention(s)
                if live(s, -2):
                    act.wait_ge(x2T_done, s - 1)
                    nc.scalar.copy(x2T[:].rearrange("p k n -> p (k n)"), bank[7][:, 0:D]).then_inc(x2T_ready, 1)
                if live(s, 2):
                    evacuate_transposes(s + 2, odd)
                if live(s, -2):
                    act.wait_ge(max_ready, s - 1)
                    nc.scalar.activation(ex[:], bank[7][:, 0:E], ACT.Exp, bias=neg_max[:],
                                         accum_out=ex_sum[:]).then_inc(exp_ready, 1)
                if live(s, 0) and not odd:
                    query_features(p, 0)
                if odd and live(s, 1):
                    add_bias(0, kT_hi, bk_s, k_done, kT_ready, p + 1)
                if live(s, -1) and not behind(s):
                    high_attention(s)
                if live(s, 0):
                    act.wait_ge(kv_done, s + 1)
                    for i in range(2):
                        lo = i * FD
                        src = bank[2][lo:lo + FD, 0:PAIRS * 2 * AUG].rearrange("p (j c) -> p j c", c=2 * AUG)
                        nc.scalar.copy(kv[lo:lo + FD, :, i * AUG:(i + 1) * AUG],
                                       src[:, :, i * AUG:(i + 1) * AUG]).then_inc(kv_ready, 1)
                if live(s, -2):
                    if live(s, -3) and rows_of(s - 2) is rows:
                        act.wait_ge(scattered, 32 * (s - 2))
                    nc.scalar.copy(rows_of(s - 2)[:, :, 0:D],
                                   xn2[:].rearrange("p (o d) -> p o d", o=1).to_broadcast([P, 2, D])).then_inc(rows_ready, 1)

            for dst, src in ((wk_s, wkT), (wv_s, wvT)):
                act.dma_start(dst, src.rearrange("(k p) n -> p k n", p=P)).then_inc(kv_w_loaded, 16)
            act.dma_start(bk_s[:], bk).then_inc(kv_w_loaded, 16)
            act.dma_start(bv_s[:], bv.to_broadcast([P, D])).then_inc(kv_w_loaded, 16)
            for dst, src in ((bq_s, bq), (mask_s, maskT)):
                act.dma_start(dst[:], src).then_inc(att_w_loaded, 16)
            high_context(0)
            evacuate_transposes(0, 0)
            evacuate_transposes(1, 1)
            act.wait_ge(kv_w_loaded, 64)
            add_bias(0, kT_hi, bk_s, k_done, kT_ready, 0)
            act.wait_ge(att_w_loaded, 80)
            act.wait_ge(consts_ready, 2)
            steps_of_attention(step, act)

            def load(t, u):
                at = act.value_load(tab_row[0:1, bass.ds(t, 1)], min_val=0, max_val=PAD_AT)
                if tile_live(t, -4):
                    act.wait_ge(meta_ready, t - 3)
                act.dma_start(x_in[:, u, :], bucket[bass.ds(at, P), :]).then_inc(x_in_loaded[u], 16)

            def evacuate_x(t):
                act.wait_ge(xT_done, t + 1)
                nc.scalar.copy(x_hi.rearrange("p k n -> p (k n)"), bank[7][:, 0:D]).then_inc(x_hi_ready, 1)

            def evacuate_y(t, v):
                act.wait_ge(y_done, t + 1)
                if tile_live(t, -4):
                    act.wait_ge(y_added, 16 * (t - 3))
                nc.scalar.activation(y[:, v, :], bank[6][:, 0:D], ACT.Copy, scale=meta[:, v, 1:2]).then_inc(y_ready, 1)

            def mix(t, u):
                if isinstance(t, int) and t == 2:
                    act.wait_ge(pad_stored[2], 16 * (E - 4))
                if tile_live(t, -2):
                    load(t + 2, (u + 2) % 4)
                for c in range(2):
                    act.wait_ge(h_done, 2 * t + (c + 1))
                    nc.scalar.activation(silu[:, c, :], bank[c][:, 0:MC], ACT.Silu).then_inc(silu_ready, 1)
                evacuate_x(t + 1)
                if tile_live(t, -1):
                    evacuate_y(t - 1, (u - 1) % 4)
                for i, (b, n) in enumerate(((4, 4), (5, MB - 4))):
                    act.wait_ge(gT_done, 2 * t + (i + 1))
                    nc.scalar.copy(g_hi[:, 4 * i:4 * i + n, :].rearrange("p k n -> p (k n)"),
                                   bank[b][:, 0:n * P]).then_inc(g_hi_ready, 1)

            nc.scalar.activation(silu_first[:], minus_half[:, 0:1], ACT.Silu)
            act.wait_ge(scattered, 32 * NT)
            act.wait_ge(pad_stored[0], 16)
            act.dma_start(x_in[:, 0, :], bucket[0:P, :]).then_inc(x_in_loaded[0], 16)
            evacuate_x(0)
            act.wait_ge(pad_stored[1], 16 * 4)
            act.wait_ge(list_ready, 3)
            for t in range(1, 4):
                load(t, t)
            act.wait_ge(list_ready, 7)
            tiles_of_mixture(act, mix)

            def drain(n, v):
                evacuate_y(n - 1, v)
                ahead = (v + 2) % 4
                act.wait_ge(x_in_loaded[ahead], 4 * (n + 1 - ahead) + 16)
                settle(act)

            last_tile(act, drain)

        @block.vector
        def _(dve):
            def statistics(a, b):
                for n in range(a, b):
                    if n in CUT:
                        dve.wait_ge(x_loaded[CUT.index(n)], 16)
                    nc.vector.bn_stats(stats[:, n, :], x_all[:, n * D:(n + 1) * D]).then_inc(stats_ready, 1)
                for n in range(a, b):
                    dve.wait_ge(stats_ready, n + 1)
                    nc.vector.bn_aggr(mv[:, n, :], stats[:, n, :]).then_inc(mv_ready, 1)

            def normalise(s):
                nc.vector.tensor_scalar(xn, x_all[:, bass.ds(s * D, D)],
                                        mv[:, bass.ds(s, 1), 0:1].rearrange("p a b -> p (a b)"),
                                        rs1[:, 4, bass.ds(s, 1)], ALU.subtract, ALU.mult).then_inc(xn_ready, 1)

            def high_piece(at, n):
                nc.vector.tensor_copy(w_hi[:, bass.ds(at, n)], raw[:, bass.ds(at, n)]).then_inc(hi_ready, 1)

            def split_weights(step_sem, done, hi, lo, of):
                nc.vector.tensor_copy(hi, of).then_inc(step_sem, 1)
                dve.wait_ge(step_sem, done + 1)
                nc.vector.tensor_tensor(lo, of, hi.bitcast(F32), ALU.subtract).then_inc(step_sem, 1)

            def low_channels(lo, hi, of, bias, ready, done, p):
                dve.wait_ge(ready, p + 1)
                for h in range(KD):
                    last = nc.vector.scalar_tensor_tensor(out=lo[:, h, :], in0=of[:, h * 2 * P:(h + 1) * 2 * P],
                                                          scalar=bias[:, h:h + 1], in1=hi[:, h, :].bitcast(F32),
                                                          op0=ALU.add, op1=ALU.subtract)
                last.then_inc(done, 1)

            statistics(0, CUT[1])
            dve.wait_ge(rs1_step, 6)
            normalise(0)
            dve.wait_ge(tr_done, 1)
            normalise(1)
            dve.wait_ge(kv_w_loaded, 64)
            split_weights(att_halves, 0, wk_hi[:], wk_lo[:], wk_s)
            split_weights(att_halves, 2, wv_hi, wv_lo, wv_s)
            dve.wait_ge(tr_done, 2)
            normalise(2)
            dve.wait_ge(att_w_loaded, 80)
            split_weights(att_halves, 4, bdk_hi[:], bdk_lo[:], bdk_s)
            low_channels(kT_lo, kT_hi, bank[0], bk_s, kT_ready, kT_lo_ready, 0)
            split_weights(att_halves, 6, bdq_hi[:], bdq_lo[:], bdq_s)
            dve.wait_ge(consts_ready, 2)

            def slots(s):
                n = 3 * (s - 3)
                dve.wait_ge(rank_done, s - 2)
                nc.vector.tensor_tensor(slot_of[:], bank[4][:, 0:E], expert_base[:], ALU.add).then_inc(slot_step, 1)
                nc.vector.tensor_tensor(counted[:], counted[:], chosen[:], ALU.add)
                dve.wait_ge(slot_step, n + 1)
                nc.vector.tensor_tensor(picked[:], slot_of[:].rearrange("p (o e) -> p o e", o=1).to_broadcast([P, 2, E]),
                                        pick[:], ALU.mult).then_inc(slot_step, 1)
                dve.wait_ge(slot_step, n + 2)
                nc.vector.tensor_reduce(slot_f[:], picked[:], AX.X, ALU.add).then_inc(slot_step, 1)
                dve.wait_ge(slot_step, n + 3)
                if rows_of(s - 3) is last_rows:
                    dve.wait_ge(scattered, 32 * (s - 3))
                nc.vector.tensor_copy(slot[:], slot_f[:]).then_inc(slot_ready, 1)

            def attend(s):
                dve.wait_ge(qkv_done, s)
                o = read_bank(s)[:, 0:NH * AUG].rearrange("p (h c) -> p h c", c=AUG)
                nc.vector.tensor_scalar(den[:].rearrange("p (h o) -> p h o", o=1), o[:, :, HD:AUG], 1e-8, None,
                                        ALU.add).then_inc(den_step, 1)
                dve.wait_ge(den_step, 2 * s - 1)
                nc.vector.reciprocal(rden[:], den[:]).then_inc(den_step, 1)
                dve.wait_ge(den_step, 2 * s)
                nc.vector.tensor_tensor(att[:], o[:, :, 0:HD], rden[:].rearrange("p (h o) -> p h o", o=1).to_broadcast([P, NH, HD]),
                                        ALU.mult).then_inc(att_ready, 1)

            def best_two(s):
                n = 8 * (s - 2)
                dve.wait_ge(exp_ready, s - 1)
                nc.vector.reciprocal(inv_sum[:], ex_sum[:]).then_inc(top_step, 1)
                dve.wait_ge(top_step, n + 1)
                nc.vector.tensor_scalar(prob[:], ex[:], inv_sum[:], None, ALU.mult).then_inc(top_step, 1)
                dve.wait_ge(top_step, n + 2)
                settle(dve)
                nc.vector.max(best[:], prob[:]).then_inc(top_step, 1)
                dve.wait_ge(top_step, n + 3)
                settle(dve)
                nc.vector.max_index(best_i[:], best[:], prob[:]).then_inc(top_step, 1)
                nc.vector.tensor_tensor(top_sum[:], best[:, 0:1], best[:, 1:2], ALU.add).then_inc(top_step, 1)

            def choices(s):
                n = 8 * (s - 2)
                dve.wait_ge(top_step, n + 4)
                nc.vector.tensor_copy(best_f[:], best_i[:, 0:2]).then_inc(top_step, 1)
                dve.wait_ge(top_step, n + 5)
                nc.vector.reciprocal(inv_top[:], top_sum[:]).then_inc(top_step, 1)
                dve.wait_ge(top_step, n + 6)
                if live(s, -3):
                    dve.wait_ge(slot_ready, s - 2)
                    if rows_of(s - 2) is rows:
                        dve.wait_ge(scattered, 32 * (s - 2))
                for k in range(2):
                    last = nc.vector.tensor_scalar(pick[:, k, :], expert_no[:], best_f[:, k:k + 1], None, ALU.is_equal)
                last.then_inc(top_step, 1)
                dve.wait_ge(top_step, n + 7)
                nc.vector.tensor_scalar(rows_of(s - 2)[:, :, D + 1:D + 2].rearrange("p k o -> p (k o)"), best[:, 0:2], inv_top[:], None, ALU.mult)
                nc.vector.tensor_copy(rows_of(s - 2)[:, :, D:D + 1].rearrange("p k o -> p (k o)").bitcast(U32),
                                      token_id[:, bass.ds(s - 2, 1)].to_broadcast([P, 2]))
                dve.wait_ge(top_step, n + 8)
                nc.vector.tensor_tensor(chosen[:], pick[:, 0, :], pick[:, 1, :], ALU.add).then_inc(chosen_ready, 1)

            def low_attention(s):
                dve.wait_ge(attT_ready, s)
                nc.vector.tensor_tensor(attT_lo[:].rearrange("p k n -> p (k n)"), bank[5][:, 0:D],
                                        attT_hi[:].rearrange("p k n -> p (k n)").bitcast(F32), ALU.subtract).then_inc(attT_lo_ready, 1)

            def residual(s):
                dve.wait_ge(proj_done, s)
                dve.wait_ge(xb_ready, s)
                if live(s, -2):
                    dve.wait_ge(x2_stored, 16 * s)
                nc.vector.tensor_tensor(x2[:], bank[3][:, 0:D], x_all[:, bass.ds((s - 1) * D, D)], ALU.add).then_inc(x2_ready, 1)
                dve.wait_ge(x2_ready, s)
                nc.vector.bn_stats(stats2[:], x2[:]).then_inc(stats2_ready, 1)
                dve.wait_ge(stats2_ready, s)
                settle(dve)
                nc.vector.bn_aggr(mv2[:], stats2[:]).then_inc(mv2_ready, 1)

            def step(s, p, odd):
                if live(s, 0):
                    dve.wait_ge(v_done, s + 1)
                    nc.vector.tensor_tensor(v_aug[:, :, 0:HD], bank[6][:, 0:D].rearrange("p (h d) -> p h d", d=HD),
                                            bv_s[:].rearrange("p (h d) -> p h d", d=HD), ALU.add).then_inc(v_ready, 1)
                if behind(s):
                    attend(s)
                    slots(s)
                    low_attention(s)
                if live(s, -3) and not behind(s):
                    slots(s)
                if live(s, -2):
                    dve.wait_ge(rs2_step, 6 * (s - 1))
                    if live(s, -3):
                        dve.wait_ge(rows_ready, s - 2)
                    nc.vector.tensor_scalar(xn2[:], x2[:], mv2[:, 0:1], rs2[:, 4:5],
                                            ALU.subtract, ALU.mult).then_inc(xn2_ready, 1)
                if live(s, 0) and not odd:
                    low_channels(qT_lo, qT_hi, bank[1], bq_s, qT_ready, qT_lo_ready, p)
                if behind(s):
                    residual(s)
                for h in range(KD):
                    if live(s, 0):
                        dve.wait_ge(kf_done, 2 * s + (h + 1))
                        nc.vector.tensor_scalar(kf[:, h * HALF:(h + 1) * HALF], bank[5 + h][:], 0.0,
                                                mask_s[:, bass.ds(s, 1)], ALU.max, ALU.mult).then_inc(kf_ready, 1)
                if live(s, -1) and not behind(s):
                    attend(s)
                if live(s, -2):
                    dve.wait_ge(logits_done, s - 1)
                    nc.vector.tensor_reduce(neg_max[:], bank[7][:, 0:E], AX.X, ALU.max, negate=True).then_inc(max_ready, 1)
                if live(s, 3):
                    dve.wait_ge(tr_done, s + 3)
                    if isinstance(s, int) and s + 3 in CUT:
                        dve.wait_ge(rs1_step, 6 * CUT.index(s + 3) + 6)
                    normalise(s + 3)
                if live(s, -2):
                    best_two(s)
                if live(s, -1) and not behind(s):
                    low_attention(s)
                if odd and live(s, 1):
                    low_channels(kT_lo, kT_hi, bank[0], bk_s, kT_ready, kT_lo_ready, p + 1)
                if live(s, -1) and not behind(s):
                    residual(s)
                if live(s, -2):
                    choices(s)

            def behind_first(s):
                statistics(CUT[s + 1], CUT[s + 2])
                if s == 0:
                    dve.wait_ge(out_w_loaded, 48)
                    split_weights(out_halves, 0, wo_hi, wo_lo, wo_s)

            steps_of_attention(step, dve, behind_first)

            done = [0]

            def link(ins):
                done[0] += 1
                ins.then_inc(list_step, 1)
                dve.wait_ge(list_step, done[0])

            def wide(a):
                return a.rearrange("a (o e) -> a o e", o=1).to_broadcast([1, TILES, E])

            dve.wait_ge(counts_done, 1)
            link(nc.vector.tensor_copy(n_row[:], bank[4][0:1, 0:E]))
            nc.vector.tensor_copy(tab_count[:], n_row[:]).then_inc(list_ready, 1)
            link(nc.vector.tensor_tensor(more, n_row[:].rearrange("a (e o) -> a e o", o=1).to_broadcast([1, E, NT]),
                                         steps[:], ALU.is_gt))
            link(nc.vector.tensor_reduce(n_tiles[:], more, AX.X, ALU.add))
            link(nc.vector.tensor_scalar(ends[:, 0, :], n_tiles[:], 1.0, None, ALU.max))
            for i, by in enumerate((1, 2, 4)):
                link(nc.vector.tensor_copy(ends[:, i + 1, 0:by], ends[:, i, 0:by]))
                link(nc.vector.tensor_tensor(ends[:, i + 1, by:E], ends[:, i, by:E], ends[:, i, 0:E - by], ALU.add))
            link(nc.vector.tensor_tensor(past, tile_no[:].rearrange("a (t o) -> a t o", o=1).to_broadcast([1, TILES, E]),
                                         wide(ends[:, 3, :]), ALU.is_ge))
            link(nc.vector.tensor_reduce(lists[:, 0, :], past, AX.X, ALU.add))
            link(nc.vector.tensor_scalar(lists[:, 1, :], lists[:, 0, :], float(E - 1), None, ALU.min))
            nc.vector.tensor_copy(tab_expert, lists[:, 1, :]).then_inc(list_ready, 1)
            link(nc.vector.tensor_scalar(n_tiles[:], ends[:, 0, :], -float(P), float(CAP), ALU.mult, ALU.add))
            link(nc.vector.tensor_tensor(skip, past, wide(n_tiles[:]), ALU.mult))
            link(nc.vector.tensor_reduce(lists[:, 2, :], skip, AX.X, ALU.add))
            link(nc.vector.scalar_tensor_tensor(out=lists[:, 3, :], in0=tile_no[:], scalar=float(P),
                                                in1=lists[:, 2, :], op0=ALU.mult, op1=ALU.add))
            link(nc.vector.tensor_scalar(lists[:, 3, :], lists[:, 3, :], float(PAD_AT), None, ALU.min))
            nc.vector.tensor_copy(tab_row, lists[:, 3, :]).then_inc(list_ready, 1)

            def split_x(t, u):
                dve.wait_ge(x_hi_ready, t + 1)
                nc.vector.tensor_tensor(x_lo.rearrange("p k n -> p (k n)"), bank[7][:, 0:D],
                                        x_hi.rearrange("p k n -> p (k n)").bitcast(F32), ALU.subtract).then_inc(x_lo_ready, 1)
                if tile_live(t, -4):
                    dve.wait_ge(y_added, 16 * (t - 3))
                nc.vector.tensor_copy(meta[:, u, :].bitcast(U32), x_in[:, u, D:ROW].bitcast(U32)).then_inc(meta_ready, 1)

            def high_halves(first, t, parts, slot_free):
                with dve.If(first):
                    e = dve.value_load(tab_expert[0:1, bass.ds(t, 1)], min_val=1, max_val=E - 2)
                    slot_free()
                    dve.wait_ge(raw_ready, e)
                    settle(dve)
                    at = dve.snap(((e + 1) % 2) * WALL)
                    for i in parts:
                        high_piece(at + i * W13, W13)

            def mix(t, u):
                if tile_live(t, -1):
                    first = dve.value_load(tab_first[0:1, bass.ds(t, 1)], min_val=0, max_val=1)
                    high_halves(first, t, (0, 1), lambda: dve.wait_ge(h_done, 2 * t))
                for c in range(2):
                    dve.wait_ge(silu_ready, 2 * t + (c + 1))
                    nc.vector.tensor_tensor(g[:, c * MC:(c + 1) * MC], bank[2 + c][:, 0:MC], silu[:, c, :],
                                            ALU.mult).then_inc(g_ready, 1)
                split_x(t + 1, (u + 1) % 4)
                for i, (b, n) in enumerate(((4, 4), (5, MB - 4))):
                    dve.wait_ge(g_hi_ready, 2 * t + (i + 1))
                    last = nc.vector.tensor_tensor(g_lo[:, 4 * i:4 * i + n, :].rearrange("p k n -> p (k n)"),
                                                   bank[b][:, 0:n * P],
                                                   g_hi[:, 4 * i:4 * i + n, :].rearrange("p k n -> p (k n)").bitcast(F32),
                                                   ALU.subtract)
                last.then_inc(g_lo_ready, 1)
                if tile_live(t, -1):
                    high_halves(first, t, (2,), lambda: dve.wait_ge(y_done, t))

            split_x(0, 0)
            link(nc.vector.tensor_scalar(active, tile_no[:], ends[:, 3, E - 1:E], None, ALU.is_lt))
            link(nc.vector.tensor_reduce(used[:, 0:1], active, AX.X, ALU.add))
            link(nc.vector.tensor_scalar(used[:, 1:2], used[:, 0:1], -float(SURE), None, ALU.add))
            link(nc.vector.tensor_tensor(is_last, active[:, 0:MOST], active[:, 1:MOST + 1], ALU.subtract))
            link(nc.vector.tensor_reduce(last_of[:], is_last.rearrange("a (j v) -> a v j", v=4), AX.X, ALU.add))
            nc.vector.tensor_copy(tab_active, active).then_inc(list_ready, 1)
            nc.vector.tensor_copy(tab_last[:], last_of[:]).then_inc(list_ready, 1)
            nc.vector.tensor_copy(tab_used[:], used[:, 1:2]).then_inc(list_ready, 1)
            link(nc.vector.memset(lists[:, 4, 0:1], 0.0))
            link(nc.vector.tensor_tensor(lists[:, 4, 1:TILES], lists[:, 1, 1:TILES], lists[:, 1, 0:TILES - 1], ALU.subtract))
            link(nc.vector.tensor_scalar(lists[:, 2, :], lists[:, 1, :], float(E - 1), None, ALU.is_lt))
            link(nc.vector.tensor_tensor(lists[:, 4, :], lists[:, 4, :], lists[:, 2, :], ALU.mult))
            nc.vector.tensor_copy(tab_first, lists[:, 4, :]).then_inc(list_ready, 1)
            dve.wait_ge(list_ready, 7)
            tiles_of_mixture(dve, mix)


def kernel(**inputs):
    import numpy as np
    import concourse.bacc as bacc
    from concourse.bass_utils import run_bass_kernel_spmd as run

    def block_diagonal(w):
        wide = np.zeros((P, HALF), w.dtype)
        for h in range(P // HD):
            wide[h * HD:(h + 1) * HD, h * FD:(h + 1) * FD] = w.T
        return wide

    i = {k: np.asarray(v) for k, v in inputs.items()}
    a = {
        "x": i["x"].reshape(T, D), "ctxT": i["ctx_2048"].reshape(T, D).T, "maskT": i["mask_BxS2_ff1"].T,
        "wqT": i["L0_xattn_Wq"].T, "bq": i["L0_xattn_bq"].reshape(KD, P).T,
        "wkT": i["L0_xattn_Wk"].T, "bk": i["L0_xattn_bk"].reshape(KD, P).T,
        "wvT": i["L0_xattn_Wv"].T, "bv": i["L0_xattn_bv"].reshape(1, D),
        "bdq": block_diagonal(i["L0_xattn_Wqf"]), "bdk": block_diagonal(i["L0_xattn_Wkf"]),
        "woT": i["L0_xattn_Wo"].T, "bo": i["L0_xattn_bo"].reshape(1, D),
        "gate": i["L0_ffn_gate_w"], "w1": i["L0_ffn_w1"], "w2": i["L0_ffn_w2"], "w3": i["L0_ffn_w3"],
    }
    a = {f"in_{k}": np.ascontiguousarray(v) for k, v in a.items()}
    nc = bacc.Bacc("TRN2", target_bir_lowering=False, num_devices=1)
    args = [nc.dram_tensor(k, v.shape, mybir.dt.from_np(v.dtype), kind="ExternalInput").ap() for k, v in a.items()]
    args.append(nc.dram_tensor("out_rows", (T + P, D), F32, kind="ExternalOutput").ap())
    build(nc, *args)
    r = run(nc, [a], core_ids=[0])
    return r.results[0]["out_rows"][0:T].reshape(NT, P, D)
```
